# Optimizing a Trainium2 kernel written in Bass

```python
import numpy as np
import jax
import jax.numpy as jnp

def _softmax(x, axis=-1):
    return jax.nn.softmax(x, axis=axis)

def _gelu(x):
    return jax.nn.gelu(x, approximate=True)

def _silu(x):
    return jax.nn.silu(x)

def _sigmoid(x):
    return jax.nn.sigmoid(x)

def _layernorm(x, axis=-1, eps=1e-05):
    m = jnp.mean(x, axis=axis, keepdims=True)
    v = jnp.var(x, axis=axis, keepdims=True)
    return (x - m) / jnp.sqrt(v + eps)

def _scatter_add(tgt, idx, src, axis=0):
    return tgt.at[idx].add(src)

def _segment_sum(src, seg, n):
    return jax.ops.segment_sum(src, seg, n)
kernel_name = 'mk_gnn_preln_d1_gnn_r64_3ee30c'

def setup_inputs(seed: int=0):
    np.random.seed(seed)
    _w = jnp.asarray

    def _rec_inputs():
        import jax
        import jax.numpy as jnp
        _gk = jax.random.key(seed)
        x = -0.000202 + 1 * jax.random.normal(jax.random.fold_in(_gk, 1), (50000, 128), jnp.float32)
        src = jax.random.randint(jax.random.fold_in(_gk, 2), (12500,), 0, 50000, jnp.int32)
        dst = jnp.minimum((50000 * jax.random.uniform(jax.random.fold_in(_gk, 3), (12500,)) ** 2.0).astype(jnp.int32), 49999)
        _o = jnp.argsort(dst, stable=True)
        src = src[_o]
        dst = dst[_o]
        edge_attr_16 = -0.00010739 + 0.99994 * jax.random.normal(jax.random.fold_in(_gk, 12), (12500, 16), jnp.float32)
        node_vec1 = jax.random.uniform(jax.random.fold_in(_gk, 13), (50000, 1), jnp.float32, 0.0, 0.999973)
        return (x, src, dst, edge_attr_16, node_vec1)
    x, src, dst, edge_attr_16, node_vec1 = _rec_inputs()

    def _L0_gnn_setup():
        import jax, jax.numpy as jnp
        import numpy as np
        import math
        N_NODES = 50000
        N_EDGES = 12500
        IN_DIM = 128
        OUT_DIM = 128
        EDGE_DIM = 16
        AVG_D_LOG = math.log(16.0)
        BN_EPS = 1e-05

        def _dgn_forward(h, e, src, dst, snorm_n, W_pre, b_pre, W_post, b_post, bn_gamma, bn_beta):
            N = h.shape[0]
            h_in = h
            z2 = jnp.concatenate([h[src], h[dst], e], axis=1)
            msg = z2 @ W_pre + b_pre
            ones = jnp.ones((msg.shape[0],), dtype=msg.dtype)
            deg = jax.ops.segment_sum(ones, dst, num_segments=N)
            s = jax.ops.segment_sum(msg, dst, num_segments=N)
            mean = s / jnp.maximum(deg, 1.0)[:, None]
            has = (deg > 0)[:, None]
            mx = jnp.where(has, jax.ops.segment_max(msg, dst, num_segments=N), 0.0)
            mn = jnp.where(has, jax.ops.segment_min(msg, dst, num_segments=N), 0.0)
            agg = jnp.concatenate([mean, mx, mn], axis=1)
            log_deg = jnp.log(deg + 1.0)[:, None]
            amp = agg * (log_deg / AVG_D_LOG)
            att = agg * (AVG_D_LOG / jnp.where(log_deg > 0, log_deg, 1.0))
            hagg = jnp.concatenate([agg, amp, att], axis=1)
            hcat = jnp.concatenate([h, hagg], axis=1)
            out = hcat @ W_post + b_post
            out = out * snorm_n
            out = out / jnp.sqrt(1.0 + BN_EPS) * bn_gamma + bn_beta
            out = jax.nn.relu(out)
            out = h_in + out
            return out
        key = jax.random.key(seed)
        ks = jax.random.split(key, 12)
        h = jax.random.normal(ks[0], (N_NODES, IN_DIM), dtype=jnp.float32)
        e = jax.random.normal(ks[1], (N_EDGES, EDGE_DIM), dtype=jnp.float32)
        src = jax.random.randint(ks[2], (N_EDGES,), 0, N_NODES, dtype=jnp.int32)
        dst = jax.random.randint(ks[3], (N_EDGES,), 0, N_NODES, dtype=jnp.int32)
        snorm_n = jax.random.uniform(ks[4], (N_NODES, 1), dtype=jnp.float32)
        pre_in = 2 * IN_DIM + EDGE_DIM
        W_pre = jax.random.normal(ks[5], (pre_in, IN_DIM), dtype=jnp.float32) / np.sqrt(pre_in)
        b_pre = jnp.zeros((IN_DIM,), dtype=jnp.float32)
        post_in = (3 * 3 + 1) * IN_DIM
        W_post = jax.random.normal(ks[6], (post_in, OUT_DIM), dtype=jnp.float32) / np.sqrt(post_in)
        b_post = jnp.zeros((OUT_DIM,), dtype=jnp.float32)
        bn_gamma = jax.random.normal(ks[7], (OUT_DIM,), dtype=jnp.float32) * 0.1 + 1.0
        bn_beta = jax.random.normal(ks[8], (OUT_DIM,), dtype=jnp.float32) * 0.1
        return {'h': h, 'e': e, 'src': src, 'dst': dst, 'snorm_n': snorm_n, 'W_pre': W_pre, 'b_pre': b_pre, 'W_post': W_post, 'b_post': b_post, 'bn_gamma': bn_gamma, 'bn_beta': bn_beta}
    _L0_gnn_all = _L0_gnn_setup()
    _L0_gnn_in = {k: v for k, v in _L0_gnn_all.items() if k in ('W_pre', 'b_pre', 'W_post', 'b_post', 'bn_gamma', 'bn_beta')}
    del _L0_gnn_all
    return {'x': x, 'src': src, 'dst': dst, 'edge_attr_16': edge_attr_16, 'node_vec1': node_vec1, 'L0_gnn_W_pre': _L0_gnn_in['W_pre'], 'L0_gnn_b_pre': _L0_gnn_in['b_pre'], 'L0_gnn_W_post': _L0_gnn_in['W_post'], 'L0_gnn_b_post': _L0_gnn_in['b_post'], 'L0_gnn_bn_gamma': _L0_gnn_in['bn_gamma'], 'L0_gnn_bn_beta': _L0_gnn_in['bn_beta']}

def reference(x, src, dst, edge_attr_16, node_vec1, L0_gnn_W_pre, L0_gnn_b_pre, L0_gnn_W_post, L0_gnn_b_post, L0_gnn_bn_gamma, L0_gnn_bn_beta):
    import jax
    import jax.numpy as jnp

    def _L0_gnn_ref(h, e, src, dst, snorm_n, W_pre, b_pre, W_post, b_post, bn_gamma, bn_beta):
        import jax, jax.numpy as jnp
        import numpy as np
        import math
        N_NODES = 50000
        N_EDGES = 12500
        IN_DIM = 128
        OUT_DIM = 128
        EDGE_DIM = 16
        AVG_D_LOG = math.log(16.0)
        BN_EPS = 1e-05

        def _dgn_forward(h, e, src, dst, snorm_n, W_pre, b_pre, W_post, b_post, bn_gamma, bn_beta):
            N = h.shape[0]
            h_in = h
            z2 = jnp.concatenate([h[src], h[dst], e], axis=1)
            msg = z2 @ W_pre + b_pre
            ones = jnp.ones((msg.shape[0],), dtype=msg.dtype)
            deg = jax.ops.segment_sum(ones, dst, num_segments=N)
            s = jax.ops.segment_sum(msg, dst, num_segments=N)
            mean = s / jnp.maximum(deg, 1.0)[:, None]
            has = (deg > 0)[:, None]
            mx = jnp.where(has, jax.ops.segment_max(msg, dst, num_segments=N), 0.0)
            mn = jnp.where(has, jax.ops.segment_min(msg, dst, num_segments=N), 0.0)
            agg = jnp.concatenate([mean, mx, mn], axis=1)
            log_deg = jnp.log(deg + 1.0)[:, None]
            amp = agg * (log_deg / AVG_D_LOG)
            att = agg * (AVG_D_LOG / jnp.where(log_deg > 0, log_deg, 1.0))
            hagg = jnp.concatenate([agg, amp, att], axis=1)
            hcat = jnp.concatenate([h, hagg], axis=1)
            out = hcat @ W_post + b_post
            out = out * snorm_n
            out = out / jnp.sqrt(1.0 + BN_EPS) * bn_gamma + bn_beta
            out = jax.nn.relu(out)
            out = h_in + out
            return out
        return _dgn_forward(h, e, src, dst, snorm_n, W_pre, b_pre, W_post, b_post, bn_gamma, bn_beta)
    h = jnp.maximum(_layernorm(x, axis=-1), 0.0)
    x = x + _L0_gnn_ref(h, edge_attr_16, src, dst, node_vec1, L0_gnn_W_pre, L0_gnn_b_pre, L0_gnn_W_post, L0_gnn_b_post, L0_gnn_bn_gamma, L0_gnn_bn_beta)
    return x

_drawn_inputs = setup_inputs


def setup_inputs(seed=0):
    import zlib

    import numpy as np

    out = dict(_drawn_inputs(seed))
    spreads = {'L0_gnn_b_pre': (0.0, 0.315), 'L0_gnn_b_post': (0.0, 0.331)}
    factors = {'L0_gnn_bn_gamma': 2.777}
    for name, (base, spread) in spreads.items():
        noise = np.random.default_rng([zlib.crc32(name.encode()), seed]).standard_normal(out[name].shape)
        drawn = base * np.exp(spread * noise) if base else spread * noise
        out[name] = jnp.asarray(drawn.astype(out[name].dtype))
    for name, factor in factors.items():
        out[name] = (out[name] * factor).astype(out[name].dtype)
    return out
```

```python
import math
from contextlib import ExitStack

import concourse.bass as bass
from concourse import mybir

F32 = mybir.dt.float32
BF16 = mybir.dt.bfloat16
I32 = mybir.dt.int32
ALU = mybir.AluOpType
ACT = mybir.ActivationFunctionType
AX_X = mybir.AxisListType.X

P = 128
N = 50000
F = 128
E = 12500
ED = 16
NB = 8
EB = 2
ROWS = NB * P
STEPS = -(-N // ROWS)
ET = EB * STEPS
EW = EB * P
EPAD = ET * P
LAST_ROW0 = N - ROWS
RING = 4
LN_EPS = 1e-5
BN_EPS = 1e-5
AVG_D_LOG = math.log(16.0)
BIG = float(2 ** 127) * (2 - 2.0 ** -7)
SKIP = 65536
GROUP_SHIFT = ROWS.bit_length() - 1
assert ET * P >= E and EPAD - E < EW and 1 << GROUP_SHIFT == ROWS

NORM, TURN, MSG, POST, SCATTER, CONFIRM = 2, 3, 4, 5, 6, 7


class Step:

    def __init__(self, q, c, looped):
        self.q, self.c, self.looped = q, c, looped

    def has(self, lag):
        return self.looped or 0 <= self.c - lag < STEPS

    def at(self, lag):
        return self.q * RING + (self.c - lag)

    def slot(self, lag):
        return (self.c - lag) % RING

    def lap(self, lag):
        return self.q + (self.c - lag) // RING

    def reused(self, lag):
        return self.looped or self.c - lag >= RING

    def after(self, lag):
        return self.looped or self.c - lag >= 1


def run_steps(engine, first_lag, last_lag, body):
    begin, end = last_lag + RING, STEPS + first_lag
    turns = (end - begin) // RING
    for c in range(first_lag, begin):
        body(Step(0, c, False))
    with engine.Fori(0, turns) as q:
        for u in range(RING):
            body(Step(q, begin + u, True))
    for c in range(begin + turns * RING, STEPS + last_lag):
        body(Step(0, c, False))


def gnn_layer(nc, x, x_s, snorm, dst_ext, dst_col, next_col, src_col, e_t,
              w_pre, b_pre, w_post, b_post, gamma, beta, out):
    with ExitStack() as ctx:
        def sb(name, shape, dt=F32):
            return ctx.enter_context(nc.sbuf_tensor(name, shape, dt))

        def ps(name, shape, dt=F32):
            return ctx.enter_context(nc.psum_tensor(name, shape, dt))

        def sem(name):
            return ctx.enter_context(nc.semaphore(name))

        def sems(name):
            return [sem(f"{name}{k}") for k in range(RING)]

        flags_dram = nc.dram_tensor("flags_dram", (3, EPAD), BF16, kind="Internal").ap()
        rdeg_dram = nc.dram_tensor("rdeg_dram", (1, EPAD), F32, kind="Internal").ap()

        ident = sb("ident", [P, P])
        ones3 = sb("ones3", [3, P], BF16)
        w_msg = sb("w_msg", [P, 2, F])
        w_edge = sb("w_edge", [ED + 1, F])
        w_raw = sb("w_raw", [P, 10, F])
        w_h = sb("w_h", [P, F])
        w_agg = sb("w_agg", [P, 3, 3, F])
        gamma_b = sb("gamma_b", [P, F])
        scale_b = sb("scale_b", [P, F])
        beta_b = sb("beta_b", [P, F])
        b_post_1 = sb("b_post_1", [1, F])
        beta_1 = sb("beta_1", [1, F])
        bias_1 = sb("bias_1", [1, 2, F])
        rest_1 = sb("rest_1", [1, 2, 2, F])
        parts_1 = sb("parts_1", [1, 3, 3, 512], BF16)
        parts = sb("parts", [3, 3, 512], BF16)
        eps_c = sb("eps_c", [P, 1])
        two_c = sb("two_c", [P, 1])

        dst_i = sb("dst_i", [ET, 3, P], I32)
        flag_f = sb("flag_f", [ET, P])
        flag_n = sb("flag_n", [ET, P])
        flag_row = sb("flag_row", [ET, 3, P], BF16)
        edge_i = sb("edge_i", [ET, P], I32)
        cand = sb("cand", [ET, P])
        local = sb("local", [ET, P])
        degree = sb("degree", [ET, 2, P])
        rdeg_row = sb("rdeg_row", [ET, P])
        scaler = sb("scaler", [ET, 3, P])
        heads = sb("heads", [ET, 2])
        heads_t = sb("heads_t", [1, 2, ET])
        carry = sb("carry", [1, ET + 1])
        top_dst = sb("top_dst", [1, STEPS])
        need_i = sb("need_i", [1, 2, STEPS], I32)
        cols_i = sb("cols_i", [P, 3, ET], I32)
        same_next = sb("same_next", [P, ET])
        index = sb("index", [P, STEPS, 3 * EB], I32)
        amp_att = sb("amp_att", [P, 2, ET])

        x_in = sb("x_in", [P, RING, NB, F])
        h_row = sb("h_row", [P, RING, NB, F])
        xh = sb("xh", [P, RING, NB, F])
        h_col = sb("h_col", [P, RING, NB, P])
        s_in = sb("s_in", [P, RING, NB])
        y_out = sb("y_out", [P, RING, NB, F])
        gather_now = sb("gather_now", [P, RING, 2 * EB], I32)
        scatter_now = sb("scatter_now", [P, RING, EB], I32)
        g_in = sb("g_in", [P, RING, 2 * EB, F + 1])
        hg_row = sb("hg_row", [P, RING, 2 * EB, F])
        hg_col = sb("hg_col", [P, RING, 2 * EB, P])
        xh_dst = sb("xh_dst", [P, RING, EB, F])
        flags = sb("flags", [P, RING, 3, EW], BF16)
        rdeg = sb("rdeg", [P, RING, EW])
        e_in = sb("e_in", [ED + 1, RING, EW])
        gain = sb("gain", [P, RING, 3, EB])
        seg_sum = sb("seg_sum", [P, RING, EW])
        seg_agg = sb("seg_agg", [P, RING, 3, EW])
        comb = sb("comb", [P, 3, EB, F])
        y_edge = sb("y_edge", [P, RING, EB, F])
        NS = NB + 2 * EB
        stats = sb("stats", [P, RING, NS, 6])
        mean2 = sb("mean2", [P, RING, NS])
        mdiff = sb("mdiff", [P, 3, NS])
        var = sb("var", [P, RING, NS])
        std = sb("std", [P, RING, NS])
        rstd = sb("rstd", [P, RING, NS])
        nmean = sb("nmean", [P, RING, NS])

        turn_e = ps("turn_e", [P, 4, P])
        turn_d = ps("turn_d", [P, NB, P])
        msg_ps = ps("msg_ps", [P, 512])
        post_d = ps("post_d", [P, NB, F])
        post_e = ps("post_e", [P, EB, 4, F])

        weights_in = sem("weights_in")
        lists_in = sem("lists_in")
        set_pool = sem("set_pool")
        set_dve = sem("set_dve")
        set_act = sem("set_act")
        set_pe = sem("set_pe")
        pool_waited = sem("pool_waited")
        heads_ready, carry_ready = sem("heads_ready"), sem("carry_ready")
        lists_ready, degree_ready = sem("lists_ready"), sem("degree_ready")
        rows_ready, scalers_ready = sem("rows_ready"), sem("scalers_ready")
        parts_ready, set_ready = sem("parts_ready"), sem("set_ready")
        spread_out = sem("spread_out")
        parts_in = sem("parts_in")
        x_loaded, s_loaded, g_loaded = sems("x_loaded"), sems("s_loaded"), sems("g_loaded")
        edge_loaded = sems("edge_loaded")
        y_stored, y_scattered = sems("y_stored"), sems("y_scattered")
        index_ready, scatter_index_ready = sem("index_ready"), sem("scatter_index_ready")
        mean_step = sem("mean_step")
        var_ready = sem("var_ready")
        std_ready = sem("std_ready")
        rstd_ready = sem("rstd_ready")
        norm_ready = sem("norm_ready")
        h_ready = sem("h_ready")
        xh_ready = sem("xh_ready")
        gain_ready = sem("gain_ready")
        turned_e, turned_d = sem("turned_e"), sem("turned_d")
        col_e_ready, col_d_ready = sem("col_e_ready"), sem("col_d_ready")
        msg_ready = sem("msg_ready")
        scanned = sem("scanned")
        agg_ready = sem("agg_ready")
        mm_d_ready = sem("mm_d_ready")
        scaled = sem("scaled")
        post_d_ready = sem("post_d_ready")
        post_e_ready = sem("post_e_ready")
        comb_step = sem("comb_step")
        y_edge_ready = sem("y_edge_ready")
        y_out_ready = sem("y_out_ready")
        dense_stored = sem("dense_stored")

        WEIGHTS = 16 * 9
        LISTS = 16 * 6

        def row0(step, lag):
            if not step.looped:
                return min(step.at(lag) * ROWS, LAST_ROW0)
            return step.at(lag) * ROWS

        block = ctx.enter_context(nc.Block())

        @block.sync
        def _(sp):
            sp.dma_start(dst_i[:, 0, :], dst_ext[0:EPAD].rearrange("(t p) -> t p", p=P)).then_inc(lists_in, 16)
            sp.dma_start(dst_i[:, 1, :], dst_ext[1:EPAD + 1].rearrange("(t p) -> t p", p=P)).then_inc(lists_in, 16)
            sp.dma_start(dst_i[:, 2, :], dst_ext[2:EPAD + 2].rearrange("(t p) -> t p", p=P)).then_inc(lists_in, 16)
            sp.dma_start(cols_i[:, 0, :], src_col).then_inc(lists_in, 16)
            sp.dma_start(cols_i[:, 1, :], dst_col).then_inc(lists_in, 16)
            sp.dma_start(cols_i[:, 2, :], next_col).then_inc(lists_in, 16)
            sp.dma_start(w_raw[:, :, :], w_post.rearrange("(b k) f -> k b f", k=P)).then_inc(weights_in, 16)
            sp.dma_start(gamma_b[:, :], gamma.rearrange("(a f) -> a f", a=1).partition_broadcast(P)).then_inc(weights_in, 16)
            sp.dma_start(beta_b[:, :], beta.rearrange("(a f) -> a f", a=1).partition_broadcast(P)).then_inc(weights_in, 16)
            sp.dma_start(b_post_1[:, :], b_post.rearrange("(a f) -> a f", a=1)).then_inc(weights_in, 16)
            sp.dma_start(beta_1[:, :], beta.rearrange("(a f) -> a f", a=1)).then_inc(weights_in, 16)
            sp.dma_start(w_msg[:, 0, :], w_pre[0:P, :]).then_inc(weights_in, 16)
            sp.dma_start(w_msg[:, 1, :], w_pre[P:2 * P, :]).then_inc(weights_in, 16)
            sp.dma_start(w_edge[0:ED, :], w_pre[2 * P:2 * P + ED, :]).then_inc(weights_in, 16)
            sp.dma_start(w_edge[ED:ED + 1, :], b_pre.rearrange("(a f) -> a f", a=1)).then_inc(weights_in, 16)
            sp.wait_ge(rows_ready, 1)
            sp.dma_start(flags_dram.rearrange("c (t p) -> t c p", p=P), flag_row[:, :, :]).then_inc(spread_out, 16)
            sp.dma_start(rdeg_dram.rearrange("a (t p) -> (a t) p", p=P), rdeg_row[:, :]).then_inc(spread_out, 16)
            sp.wait_ge(parts_ready, 1)
            sp.dma_start(parts[:, :, :], parts_1[0:1, :, :, :].rearrange("a k c f -> a k (c f)")).then_inc(parts_in, 16)

            def body(t):
                if t.has(0):
                    k = t.slot(0)
                    if t.reused(0):
                        sp.wait_ge(rows_ready, 1)
                        sp.wait_ge(xh_ready, t.at(0) - RING + 1)
                    sp.dma_start(x_in[:, k, :, :],
                                 x[bass.ds(row0(t, 0), ROWS), :].rearrange("(p r) f -> p r f", p=P)
                                 ).then_inc(x_loaded[k], 16)
                if t.has(NORM):
                    k = t.slot(NORM)
                    if t.reused(NORM):
                        sp.wait_ge(rows_ready, 1)
                        sp.wait_ge(scaled, t.at(NORM) - RING + 1)
                        sp.wait_ge(agg_ready, t.at(NORM) - RING + 1)
                    elif t.c == NORM:
                        sp.wait_ge(spread_out, 32)
                    sp.dma_start(s_in[:, k, :],
                                 snorm[bass.ds(row0(t, NORM), ROWS), :].rearrange("(p r) a -> p (r a)", p=P)
                                 ).then_inc(s_loaded[k], 16)
                    e0 = t.at(NORM) * EW
                    sp.dma_start(flags[:, k, :, :],
                                 flags_dram[:, bass.ds(e0, EW)].partition_broadcast(P)).then_inc(edge_loaded[k], 16)
                    sp.dma_start(rdeg[:, k, :],
                                 rdeg_dram[:, bass.ds(e0, EW)].partition_broadcast(P)).then_inc(edge_loaded[k], 16)
                    sp.dma_start(e_in[0:ED, k, :], e_t[:, bass.ds(e0, EW)]).then_inc(edge_loaded[k], 16)
                if t.has(POST):
                    k = t.slot(POST)
                    sp.wait_ge(y_out_ready, t.at(POST) + 1)
                    if not t.looped and t.c - POST == STEPS - 1:
                        sp.wait_ge(y_stored[(k - 1) % RING], 16 * (t.lap(POST + 1) + 1))
                    sp.dma_start(out[bass.ds(row0(t, POST), ROWS), :].rearrange("(p r) f -> p r f", p=P),
                                 y_out[:, k, :, :]).then_inc(y_stored[k], 16)
                if t.has(CONFIRM):
                    sp.wait_ge(rows_ready, 1)
                    sp.wait_ge(y_stored[t.slot(CONFIRM)], 16 * (t.lap(CONFIRM) + 1))
                    sp.sem_inc(dense_stored, 1)

            run_steps(sp, 0, CONFIRM, body)

        @block.gpsimd
        def _(pool):
            pool.memset(ident[:, :], 0.0).then_inc(set_pool, 1)
            pool.wait_ge(set_pool, 1)
            pool.affine_select(out=ident[:, :], in_=ident[:, :], compare_op=ALU.not_equal, fill=1.0,
                               base=0, pattern=[[-1, P]], channel_multiplier=1).then_inc(set_pool, 1)
            pool.iota(edge_i[:, :], pattern=[[1, P]], base=0, channel_multiplier=P).then_inc(set_pool, 1)
            pool.wait_ge(lists_ready, 1)

            def body(t):
                if t.has(0):
                    k = t.slot(0)
                    if t.reused(0):
                        pool.wait_ge(gain_ready, t.at(0) - RING + 1)
                        pool.wait_ge(xh_ready, t.at(0) - RING + 1)
                    pool.tensor_copy(gather_now[:, k, :], index[:, bass.ds(t.at(0), 1), 0:2 * EB].rearrange("p a c -> p (a c)")
                                     ).then_inc(index_ready, 1)
                    pool.wait_ge(index_ready, t.at(0) + 1)
                    pool.sem_inc(pool_waited, 1)
                    for c in range(2 * EB):
                        pool.indirect_dma_start(g_in[:, k, c, :], None, x_s,
                                                bass.IndirectOffsetOnAxis(gather_now[:, k, c:c + 1], 0),
                                                ).then_inc(g_loaded[k], 16)
                if t.has(SCATTER):
                    k = t.slot(SCATTER)
                    need = pool.value_load(need_i[0:1, 1, bass.ds(t.at(SCATTER), 1)], min_val=1, max_val=STEPS)
                    if t.reused(SCATTER):
                        pool.wait_ge(y_scattered[k], 32 * t.lap(SCATTER))
                    pool.tensor_copy(scatter_now[:, k, :], index[:, bass.ds(t.at(SCATTER), 1), 2 * EB:3 * EB].rearrange("p a c -> p (a c)")
                                     ).then_inc(scatter_index_ready, 1)
                    pool.wait_ge(scatter_index_ready, t.at(SCATTER) + 1)
                    pool.wait_ge(y_edge_ready, t.at(SCATTER) + 1)
                    pool.wait_ge(dense_stored, need)
                    pool.sem_inc(pool_waited, 1)
                    for c in range(EB):
                        pool.indirect_dma_start(out, bass.IndirectOffsetOnAxis(scatter_now[:, k, c:c + 1], 0),
                                                y_edge[:, k, c, :], None, bounds_check=N - 1, oob_is_err=False,
                                                ).then_inc(y_scattered[k], 16)

            run_steps(pool, 0, SCATTER, body)
            for k in range(RING):
                pool.wait_ge(y_scattered[k], 32 * len(range(k, STEPS, RING)))
            pool.wait_ge(dense_stored, STEPS)

        @block.tensor
        def _(pe):
            pe.wait_ge(set_pool, 2)
            pe.wait_ge(heads_ready, 1)
            pe.transpose(msg_ps[0:1, 0:ET], heads[:, 0:1], ident[0:ET, 0:ET])
            pe.transpose(msg_ps[0:1, P:P + ET], heads[:, 1:2], ident[0:ET, 0:ET]).then_inc(set_pe, 1)
            pe.wait_ge(carry_ready, 1)
            pe.transpose(msg_ps[0:ET, 2 * P:2 * P + 1], carry[0:1, 0:ET], ident[0:1, 0:1]).then_inc(set_pe, 1)
            pe.wait_ge(scalers_ready, 1)
            pe.transpose(msg_ps[:, 0:ET], scaler[:, 1, :], ident[0:ET, 0:ET])
            pe.transpose(msg_ps[:, P:P + ET], scaler[:, 2, :], ident[0:ET, 0:ET]).then_inc(set_pe, 1)
            pe.wait_ge(set_ready, 1)
            pe.wait_ge(parts_in, 16)
            pe.wait_ge(weights_in, WEIGHTS)

            def body(t):
                if t.has(POST):
                    k = t.slot(POST)
                    pe.wait_ge(agg_ready, t.at(POST) + 1)
                    if t.after(POST):
                        pe.wait_ge(y_edge_ready, t.at(POST))
                    for c in range(EB):
                        o = post_e[:, c, 0:3, :]
                        pe.matmul(o, ones3[:, :], parts[:, 1, 0:3 * F], start=True, stop=False, skip_group_check=True)
                        pe.matmul(post_e[:, c, 0, :], hg_col[:, k, EB + c, :], w_h[:, :], start=False, stop=False,
                                  skip_group_check=True)
                        for a in range(3):
                            last = pe.matmul(o, seg_agg[:, k, a, c * P:(c + 1) * P], w_agg[:, a, :, :],
                                             start=False, stop=(a == 2), skip_group_check=True)
                    last.then_inc(post_e_ready, 1)
                    pe.wait_ge(scaled, t.at(POST) + 1)
                    for b in range(NB // 4):
                        last = pe.matmul(post_d[:, 4 * b:4 * b + 4, :], ones3[:, :], parts[:, 2, :],
                                         start=False, stop=True, skip_group_check=True)
                    last.then_inc(post_d_ready, 1)
                if t.has(MSG):
                    k = t.slot(MSG)
                    pe.wait_ge(col_e_ready, t.at(MSG) + 1)
                    pe.wait_ge(edge_loaded[k], 48 * (t.lap(MSG) + 1))
                    if t.after(MSG):
                        pe.wait_ge(agg_ready, t.at(MSG))
                    pe.matmul(msg_ps[:, 0:EW], w_msg[:, 0, :], hg_col[:, k, 0:EB, :], start=True, stop=False)
                    pe.matmul(msg_ps[:, 0:EW], w_msg[:, 1, :], hg_col[:, k, EB:2 * EB, :], start=False, stop=False)
                    pe.matmul(msg_ps[:, 0:EW], w_edge[:, :], e_in[:, k, :], start=False, stop=True
                              ).then_inc(msg_ready, 1)
                    pe.wait_ge(col_d_ready, t.at(MSG) + 1)
                    if t.after(MSG):
                        pe.wait_ge(y_out_ready, t.at(MSG))
                    for b in range(NB // 4):
                        pe.matmul(post_d[:, 4 * b:4 * b + 4, :], ones3[:, :], parts[:, 0, :],
                                  start=True, stop=False, skip_group_check=True)
                        for j in range(4 * b, 4 * b + 4):
                            last = pe.matmul(post_d[:, j, :], h_col[:, k, j, :], w_h[:, :],
                                             start=False, stop=(j % 4 == 3), skip_group_check=True)
                    last.then_inc(mm_d_ready, 1)
                if t.has(TURN):
                    k = t.slot(TURN)
                    pe.wait_ge(h_ready, t.at(TURN) + 1)
                    if t.after(TURN):
                        pe.wait_ge(col_e_ready, t.at(TURN))
                        pe.wait_ge(col_d_ready, t.at(TURN))
                    for c in range(2 * EB):
                        last = pe.transpose(turn_e[:, c, :], hg_row[:, k, c, :], ident[:, :])
                    last.then_inc(turned_e, 1)
                    for j in range(NB):
                        last = pe.transpose(turn_d[:, j, :], h_row[:, k, j, :], ident[:, :])
                    last.then_inc(turned_d, 1)

            run_steps(pe, TURN, POST, body)

        @block.scalar
        def _(act):
            act.wait_ge(degree_ready, 1)
            nc.scalar.activation(scaler[:, 0, :], degree[:, 0, :], ACT.Ln, bias=two_c[0:ET, 0:1]).then_inc(set_act, 1)
            act.wait_ge(set_act, 1)

            def body(t):
                if t.has(MSG):
                    k = t.slot(MSG)
                    act.wait_ge(turned_e, t.at(MSG) + 1)
                    nc.scalar.activation(hg_col[:, k, :, :], turn_e[:, :, :], ACT.Copy).then_inc(col_e_ready, 1)
                if t.has(POST):
                    k = t.slot(POST)
                    act.wait_ge(s_loaded[k], 16 * (t.lap(POST) + 1))
                    act.wait_ge(mm_d_ready, t.at(POST) + 1)
                    for j in range(NB):
                        last = nc.scalar.activation(post_d[:, j, :], post_d[:, j, :], ACT.Copy, scale=s_in[:, k, j:j + 1])
                    last.then_inc(scaled, 1)
                if t.has(NORM):
                    k = t.slot(NORM)
                    act.wait_ge(var_ready, t.at(NORM) + 1)
                    nc.scalar.activation(std[:, k, :], var[:, k, :], ACT.Sqrt, bias=eps_c[:, 0:1], scale=1.0 / F
                                         ).then_inc(std_ready, 1)
                if t.has(MSG):
                    k = t.slot(MSG)
                    act.wait_ge(turned_d, t.at(MSG) + 1)
                    for b in range(NB // 4):
                        last = nc.scalar.activation(h_col[:, k, 4 * b:4 * b + 4, :], turn_d[:, 4 * b:4 * b + 4, :], ACT.Copy)
                    last.then_inc(col_d_ready, 1)
                if t.has(NORM):
                    k = t.slot(NORM)
                    act.wait_ge(norm_ready, t.at(NORM) + 1)
                    if t.reused(NORM):
                        act.wait_ge(xh_ready, t.at(NORM) - RING + 1)
                        act.wait_ge(turned_d, t.at(NORM) - RING + 1)
                    for c in range(2 * EB):
                        nc.scalar.activation(hg_row[:, k, c, :], g_in[:, k, c, 0:F], ACT.Relu,
                                             bias=nmean[:, k, NB + c:NB + c + 1], scale=rstd[:, k, NB + c:NB + c + 1])
                    for j in range(NB):
                        last = nc.scalar.activation(h_row[:, k, j, :], x_in[:, k, j, :], ACT.Relu,
                                                    bias=nmean[:, k, j:j + 1], scale=rstd[:, k, j:j + 1])
                    last.then_inc(h_ready, 1)

            run_steps(act, NORM, POST, body)

        @block.vector
        def _(dve):
            done = [0]

            def then(ins):
                done[0] += 1
                return ins.then_inc(set_dve, 1)

            def chain(ins):
                then(ins)
                dve.wait_ge(set_dve, done[0])

            def mark(reached):
                dve.wait_ge(set_dve, done[0])
                dve.sem_inc(reached, 1)

            then(dve.memset(ones3[:, :], 1.0))
            then(dve.memset(eps_c[:, :], LN_EPS))
            then(dve.memset(two_c[:, :], 2.0))
            then(dve.memset(e_in[:, :, :], 1.0))
            then(dve.memset(parts_1[:, :, :, :], 0.0))
            then(dve.memset(seg_sum[:, RING - 1, EW - 1:EW], 0.0))
            then(dve.memset(seg_agg[:, RING - 1, :, EW - 1:EW], 0.0))
            chain(dve.memset(carry[:, :], 0.0))
            dve.wait_ge(lists_in, LISTS)
            def pairs(a):
                return a.rearrange("p (j c) -> p j c", c=EB)
            then(dve.tensor_copy(index[:, :, 0:EB], pairs(cols_i[:, 0, :])))
            then(dve.tensor_scalar(index[:, :, EB:2 * EB], pairs(cols_i[:, 1, :]), 0.0, None, ALU.max))
            chain(dve.tensor_tensor(same_next[:, :], cols_i[:, 1, :], cols_i[:, 2, :], ALU.is_equal))
            then(dve.scalar_tensor_tensor(out=index[:, :, 2 * EB:3 * EB], in0=pairs(same_next[:, :]), scalar=float(SKIP),
                                          in1=pairs(cols_i[:, 1, :]), op0=ALU.mult, op1=ALU.add))
            chain(dve.tensor_tensor(flag_f[:, :], dst_i[:, 0, :], dst_i[:, 1, :], ALU.is_equal))
            then(dve.tensor_copy(flag_row[:, 0, :], flag_f[:, :]))
            chain(dve.tensor_scalar(flag_n[:, :], flag_f[:, :], -1.0, BIG, ALU.add, ALU.mult))
            chain(dve.scalar_tensor_tensor(out=local[:, :], in0=flag_f[:, :], scalar=BIG, in1=flag_n[:, :],
                                           op0=ALU.mult, op1=ALU.add))
            then(dve.tensor_copy(flag_row[:, 1, :], local[:, :]))
            chain(dve.tensor_scalar(flag_row[:, 2, :], local[:, :], -1.0, None, ALU.mult))
            dve.wait_ge(set_pool, 3)
            chain(dve.scalar_tensor_tensor(out=flag_n[:, :], in0=flag_f[:, :], scalar=1.0, in1=edge_i[:, :],
                                           op0=ALU.is_lt, op1=ALU.mult))
            chain(dve.tensor_tensor_scan(local[:, :], flag_n[:, :], flag_n[:, :], 0.0, ALU.max, ALU.max))
            then(dve.tensor_copy(heads[:, 0:1], local[:, P - 1:P]))
            chain(dve.tensor_reduce(heads[:, 1:2], dst_i[:, 1, :], AX_X, ALU.max))
            mark(heads_ready)
            dve.wait_ge(set_pe, 1)
            chain(dve.tensor_copy(heads_t[:, :, :], msg_ps[0:1, 0:2 * P].rearrange("a (b t) -> a b t", b=2)[:, :, 0:ET]))
            chain(dve.tensor_tensor_scan(carry[0:1, 1:ET + 1], heads_t[:, 0, :], heads_t[:, 0, :], 0.0, ALU.max, ALU.max))
            mark(carry_ready)
            chain(dve.tensor_reduce(top_dst[:, :], heads_t[:, 1, :].rearrange("a (j c) -> a j c", c=EB), AX_X, ALU.max))
            chain(dve.tensor_scalar(need_i[:, 0, :], top_dst[:, :], float(STEPS * ROWS - N + ROWS), None, ALU.add))
            then(dve.tensor_scalar(need_i[:, 1, :], need_i[:, 0, :], GROUP_SHIFT, None, ALU.logical_shift_right))
            mark(lists_ready)
            dve.wait_ge(set_pe, 2)
            chain(dve.tensor_scalar(cand[:, :], local[:, :], msg_ps[0:ET, 2 * P:2 * P + 1], None, ALU.max))
            chain(dve.tensor_tensor(degree[:, 0, :], edge_i[:, :], cand[:, :], ALU.subtract))
            mark(degree_ready)
            chain(dve.tensor_scalar(degree[:, 1, :], degree[:, 0, :], 1.0, None, ALU.add))
            chain(dve.reciprocal(rdeg_row[:, :], degree[:, 1, :]))
            mark(rows_ready)
            dve.wait_ge(set_act, 1)
            then(dve.tensor_scalar(scaler[:, 1, :], scaler[:, 0, :], 1.0 / AVG_D_LOG, None, ALU.mult))
            chain(dve.reciprocal(cand[:, :], scaler[:, 0, :]))
            chain(dve.tensor_scalar(scaler[:, 2, :], cand[:, :], AVG_D_LOG, None, ALU.mult))
            mark(scalers_ready)
            dve.wait_ge(weights_in, WEIGHTS)
            chain(dve.tensor_scalar(scale_b[:, :], gamma_b[:, :], 1.0 / math.sqrt(1.0 + BN_EPS), None, ALU.mult))
            then(dve.tensor_tensor(w_h[:, :], w_raw[:, 0, :], scale_b[:, :], ALU.mult))
            for a in range(3):
                for c in range(3):
                    then(dve.tensor_tensor(w_agg[:, a, c, :], w_raw[:, 1 + 3 * c + a, :], scale_b[:, :], ALU.mult))
            then(dve.tensor_tensor(bias_1[:, 0, :], b_post_1[:, :], scale_b[0:1, :], ALU.mult))
            chain(dve.tensor_copy(bias_1[:, 1, :], beta_1[:, :]))
            src = bias_1[:, :, :]
            for k in range(3):
                chain(dve.tensor_copy(parts_1[:, k, 1, 0:F], src[:, 0, :]))
                chain(dve.tensor_copy(parts_1[:, k, 2, 0:F], src[:, 1, :]))
                if k < 2:
                    then(dve.tensor_tensor(rest_1[:, k, 0, :], src[:, 0, :], parts_1[:, k, 1, 0:F], ALU.subtract))
                    chain(dve.tensor_tensor(rest_1[:, k, 1, :], src[:, 1, :], parts_1[:, k, 2, 0:F], ALU.subtract))
                    src = rest_1[:, k, :, :]
            for k in range(3):
                for r in range(4):
                    then(dve.tensor_copy(parts_1[:, k, 0, r * F:(r + 1) * F], parts_1[:, k, 1, 0:F]))
                    if r:
                        then(dve.tensor_copy(parts_1[:, k, 2, r * F:(r + 1) * F], parts_1[:, k, 2, 0:F]))
            mark(parts_ready)
            dve.wait_ge(set_pe, 3)
            chain(dve.tensor_copy(amp_att[:, :, :], msg_ps[:, 0:2 * P].rearrange("p (b t) -> p b t", b=2)[:, :, 0:ET]))
            mark(set_ready)

            def body(t):
                if t.has(NORM):
                    k = t.slot(NORM)
                    dve.wait_ge(x_loaded[k], 16 * (t.lap(NORM) + 1))
                    for j in range(NB):
                        dve.bn_stats(stats[:, k, j, :], x_in[:, k, j, :])
                    dve.wait_ge(g_loaded[k], 32 * EB * (t.lap(NORM) + 1))
                    for c in range(2 * EB):
                        last = dve.bn_stats(stats[:, k, NB + c, :], g_in[:, k, c, 0:F])
                    last.then_inc(mean_step, 1)
                    dve.wait_ge(mean_step, 3 * t.at(NORM) + 1)
                    dve.tensor_tensor(mdiff[:, 0, :], stats[:, k, :, 1], stats[:, k, :, 4], ALU.subtract)
                    dve.tensor_tensor(mean2[:, k, :], stats[:, k, :, 1], stats[:, k, :, 4], ALU.add)
                    dve.tensor_tensor(mdiff[:, 1, :], stats[:, k, :, 2], stats[:, k, :, 5], ALU.add).then_inc(mean_step, 1)
                    dve.wait_ge(mean_step, 3 * t.at(NORM) + 2)
                    dve.tensor_tensor(mdiff[:, 2, :], mdiff[:, 0, :], mdiff[:, 0, :], ALU.mult).then_inc(mean_step, 1)
                    dve.wait_ge(mean_step, 3 * t.at(NORM) + 3)
                    dve.scalar_tensor_tensor(out=var[:, k, :], in0=mdiff[:, 2, :], scalar=F / 4.0, in1=mdiff[:, 1, :],
                                             op0=ALU.mult, op1=ALU.add).then_inc(var_ready, 1)
                if t.has(TURN):
                    k = t.slot(TURN)
                    dve.wait_ge(h_ready, t.at(TURN) + 1)
                    dve.tensor_tensor(xh_dst[:, k, :, :], g_in[:, k, EB:2 * EB, 0:F], hg_row[:, k, EB:2 * EB, :], ALU.add)
                    tiles = bass.ds(t.at(TURN) * EB, EB)
                    dve.tensor_copy(gain[:, k, 0, :], g_in[:, k, EB:2 * EB, F])
                    dve.tensor_tensor(gain[:, k, 1, :], g_in[:, k, EB:2 * EB, F], amp_att[:, 0, tiles], ALU.mult)
                    dve.tensor_tensor(gain[:, k, 2, :], g_in[:, k, EB:2 * EB, F], amp_att[:, 1, tiles], ALU.mult
                                      ).then_inc(gain_ready, 1)
                if t.has(NORM):
                    k = t.slot(NORM)
                    dve.wait_ge(std_ready, t.at(NORM) + 1)
                    dve.reciprocal(rstd[:, k, :], std[:, k, :]).then_inc(rstd_ready, 1)
                    dve.wait_ge(rstd_ready, t.at(NORM) + 1)
                    dve.scalar_tensor_tensor(out=nmean[:, k, :], in0=mean2[:, k, :], scalar=-0.5, in1=rstd[:, k, :],
                                             op0=ALU.mult, op1=ALU.mult).then_inc(norm_ready, 1)
                if t.has(TURN):
                    k = t.slot(TURN)
                    dve.tensor_tensor(xh[:, k, :, :], x_in[:, k, :, :], h_row[:, k, :, :], ALU.add).then_inc(xh_ready, 1)
                if t.has(POST):
                    k = t.slot(POST)
                    dve.wait_ge(post_d_ready, t.at(POST) + 1)
                    dve.wait_ge(xh_ready, t.at(POST) + 1)
                    if t.reused(POST):
                        dve.wait_ge(y_stored[k], 16 * t.lap(POST))
                    for b in range(NB // 4):
                        rows = slice(4 * b, 4 * b + 4)
                        last = dve.scalar_tensor_tensor(out=y_out[:, k, rows, :], in0=post_d[:, rows, :], scalar=0.0,
                                                        in1=xh[:, k, rows, :], op0=ALU.max, op1=ALU.add)
                    last.then_inc(y_out_ready, 1)
                if t.has(POST):
                    k = t.slot(POST)
                    dve.wait_ge(post_e_ready, t.at(POST) + 1)
                    dve.wait_ge(gain_ready, t.at(POST) + 1)
                    if t.reused(POST):
                        dve.wait_ge(y_scattered[k], 32 * t.lap(POST))
                    for a in range(3):
                        for c in range(EB):
                            last = dve.scalar_tensor_tensor(
                                out=comb[:, a, c, :], in0=post_e[:, c, a, :], scalar=gain[:, k, a, c:c + 1],
                                in1=comb[:, a - 1, c, :] if a else beta_b[:, :], op0=ALU.mult, op1=ALU.add)
                        last.then_inc(comb_step, 1)
                        dve.wait_ge(comb_step, 3 * t.at(POST) + a + 1)
                    dve.scalar_tensor_tensor(out=y_edge[:, k, :, :], in0=comb[:, 2, :, :], scalar=0.0,
                                             in1=xh_dst[:, k, :, :], op0=ALU.max, op1=ALU.add).then_inc(y_edge_ready, 1)
                if t.has(MSG):
                    k, before = t.slot(MSG), t.slot(MSG + 1)
                    dve.wait_ge(msg_ready, t.at(MSG) + 1)
                    dve.wait_ge(edge_loaded[k], 48 * (t.lap(MSG) + 1))
                    if t.after(MSG):
                        dve.wait_ge(agg_ready, t.at(MSG))
                    end = slice(EW - 1, EW)
                    dve.tensor_tensor_scan(seg_sum[:, k, :], flags[:, k, 0, :], msg_ps[:, 0:EW],
                                           seg_sum[:, before, end], ALU.mult, ALU.add).then_inc(scanned, 1)
                    dve.tensor_tensor_scan(seg_agg[:, k, 1, :], flags[:, k, 1, :], msg_ps[:, 0:EW],
                                           seg_agg[:, before, 1, end], ALU.min, ALU.max)
                    dve.tensor_tensor_scan(seg_agg[:, k, 2, :], flags[:, k, 2, :], msg_ps[:, 0:EW],
                                           seg_agg[:, before, 2, end], ALU.max, ALU.min)
                    dve.wait_ge(scanned, t.at(MSG) + 1)
                    dve.tensor_tensor(seg_agg[:, k, 0, :], seg_sum[:, k, :], rdeg[:, k, :], ALU.mult).then_inc(agg_ready, 1)

            run_steps(dve, NORM, POST, body)


def kernel(x, src, dst, edge_attr_16, node_vec1, L0_gnn_W_pre, L0_gnn_b_pre, L0_gnn_W_post, L0_gnn_b_post,
           L0_gnn_bn_gamma, L0_gnn_bn_beta):
    import numpy as np
    import concourse.bacc as bacc
    from concourse.bass_utils import run_bass_kernel_spmd

    x, src, dst, e, s = (np.ascontiguousarray(a) for a in (x, src, dst, edge_attr_16, node_vec1))
    dst_ext = np.full(EPAD + 2, -1, dst.dtype)
    dst_ext[1:E + 1] = dst
    src_pad = np.zeros(EPAD, src.dtype)
    src_pad[:E] = src
    e_t = np.zeros((ED, EPAD), e.dtype)
    e_t[:, :E] = e.T

    def by_slot(a):
        return np.ascontiguousarray(a.reshape(ET, P).T)

    arrays = {
        "x": x, "x_s": np.ascontiguousarray(np.concatenate([x, s], axis=1)), "snorm": s, "dst_ext": dst_ext,
        "dst_col": by_slot(dst_ext[1:EPAD + 1]), "next_col": by_slot(dst_ext[2:EPAD + 2]), "src_col": by_slot(src_pad),
        "e_t": e_t, "w_pre": L0_gnn_W_pre, "b_pre": L0_gnn_b_pre, "w_post": L0_gnn_W_post, "b_post": L0_gnn_b_post,
        "gamma": L0_gnn_bn_gamma, "beta": L0_gnn_bn_beta,
    }
    arrays = {name: np.ascontiguousarray(a) for name, a in arrays.items()}
    nc = bacc.Bacc("TRN2", target_bir_lowering=False, num_devices=1)
    args = [nc.dram_tensor(name, a.shape, mybir.dt.from_np(a.dtype), kind="ExternalInput").ap()
            for name, a in arrays.items()]
    out = nc.dram_tensor("out", (N, F), F32, kind="ExternalOutput").ap()
    gnn_layer(nc, *args, out)
    return run_bass_kernel_spmd(nc, [arrays], core_ids=[0]).results[0]["out"]
```

```python
import math
from contextlib import ExitStack

import concourse.bass as bass
from concourse import mybir

F32 = mybir.dt.float32
BF16 = mybir.dt.bfloat16
I32 = mybir.dt.int32
ALU = mybir.AluOpType
ACT = mybir.ActivationFunctionType
AX_X = mybir.AxisListType.X

P = 128
N = 50000
F = 128
E = 12500
ED = 16
NB = 8
EB = 2
ROWS = NB * P
STEPS = -(-N // ROWS)
ET = EB * STEPS
EW = EB * P
EPAD = ET * P
LAST_ROW0 = N - ROWS
RING = 4
LN_EPS = 1e-5
BN_EPS = 1e-5
AVG_D_LOG = math.log(16.0)
BIG = float(2 ** 127) * (2 - 2.0 ** -7)
PAD = 65535
SKIP = 65536
GROUP_SHIFT = ROWS.bit_length() - 1
S_COLS = 400
S_ROWS = N // S_COLS
assert S_ROWS * S_COLS == N and S_ROWS <= P
assert ET * P >= E and EPAD - E < EW and 1 << GROUP_SHIFT == ROWS

NORM, TURN, MSG, POST, CONFIRM, SCATTER = 2, 3, 4, 5, 6, 7
AHEAD = SCATTER - CONFIRM + 1


class Step:

    def __init__(self, q, c, looped):
        self.q, self.c, self.looped = q, c, looped

    def has(self, lag):
        return self.looped or 0 <= self.c - lag < STEPS

    def at(self, lag):
        return self.q * RING + (self.c - lag)

    def slot(self, lag):
        return (self.c - lag) % RING

    def lap(self, lag):
        return self.q + (self.c - lag) // RING

    def reused(self, lag):
        return self.looped or self.c - lag >= RING

    def after(self, lag):
        return self.looped or self.c - lag >= 1


def run_steps(engine, first_lag, last_lag, body):
    begin, end = last_lag + RING, STEPS + first_lag
    turns = (end - begin) // RING
    for c in range(first_lag, begin):
        body(Step(0, c, False))
    with engine.Fori(0, turns) as q:
        for u in range(RING):
            body(Step(q, begin + u, True))
    for c in range(begin + turns * RING, STEPS + last_lag):
        body(Step(0, c, False))


def gnn_layer(nc, x, x_s, snorm, dst_ext, dst_col, next_col, src_col, e_t, e_row,
              w_pre, b_pre, w_post, b_post, gamma, beta, out):
    with ExitStack() as ctx:
        def sb(name, shape, dt=F32):
            return ctx.enter_context(nc.sbuf_tensor(name, shape, dt))

        def ps(name, shape, dt=F32):
            return ctx.enter_context(nc.psum_tensor(name, shape, dt))

        def sem(name):
            return ctx.enter_context(nc.semaphore(name))

        def sems(name):
            return [sem(f"{name}{k}") for k in range(RING)]

        flags_dram = nc.dram_tensor("flags_dram", (3, EPAD), BF16, kind="Internal").ap()
        e_dram = nc.dram_tensor("e_dram", (ED, EPAD), F32, kind="Internal").ap()
        late_dram = nc.dram_tensor("late_dram", (STEPS, P, EB * F), F32, kind="Internal").ap()
        sorted_dram = nc.dram_tensor("sorted_dram", (EPAD + 2, ED + 2), F32, kind="Internal").ap()
        rdeg_dram = nc.dram_tensor("rdeg_dram", (1, EPAD), F32, kind="Internal").ap()
        s_dram = nc.dram_tensor("s_dram", (3, 3, N), BF16, kind="Internal").ap()

        ident = sb("ident", [P, P])
        ones3 = sb("ones3", [3, P], BF16)
        w_msg = sb("w_msg", [P, 2, F])
        w_edge = sb("w_edge", [ED + 1, F])
        w_raw = sb("w_raw", [P, 10, F])
        w_h = sb("w_h", [P, F])
        w_agg = sb("w_agg", [P, 3, 3, F])
        gamma_b = sb("gamma_b", [P, F])
        scale_b = sb("scale_b", [P, F])
        beta_b = sb("beta_b", [P, F])
        b_post_1 = sb("b_post_1", [1, F])
        beta_1 = sb("beta_1", [1, F])
        bias_1 = sb("bias_1", [1, 2, F])
        rest_1 = sb("rest_1", [1, 2, 2, F])
        parts_1 = sb("parts_1", [1, 2, 3, F], BF16)
        bias3 = sb("bias3", [3, F], BF16)
        add12 = sb("add12", [12, F], BF16)
        eps_c = sb("eps_c", [P, 1])
        two_c = sb("two_c", [P, 1])
        sqrt_table = sb("sqrt_table", [P, 1])

        dst_i = sb("dst_i", [ET, 3, P], I32)
        flag_f = sb("flag_f", [ET, P])
        flag_n = sb("flag_n", [ET, P])
        flag_row = sb("flag_row", [ET, 3, P], BF16)
        edge_i = sb("edge_i", [ET, P], I32)
        cand = sb("cand", [ET, P])
        local = sb("local", [ET, P])
        degree = sb("degree", [ET, 2, P])
        rdeg_row = sb("rdeg_row", [ET, P])
        scaler = sb("scaler", [ET, 3, P])
        heads = sb("heads", [ET, 2])
        heads_t = sb("heads_t", [1, 2, ET])
        carry = sb("carry", [1, ET + 1])
        top_dst = sb("top_dst", [1, STEPS])
        need_i = sb("need_i", [1, 2, STEPS], I32)
        late_f = sb("late_f", [1, STEPS + 1])
        late_i = sb("late_i", [1, STEPS + 1], I32)
        cols_i = sb("cols_i", [P, 3, ET], I32)
        same_next = sb("same_next", [P, ET])
        index = sb("index", [P, STEPS, 3 * EB], I32)
        amp_att = sb("amp_att", [P, 2, ET])

        x_in = sb("x_in", [P, RING, NB, F])
        work = sb("work", [P, 4, RING, NB, F])
        h_row, xh, h_col, y_out = work[:, 0], work[:, 1], work[:, 2], work[:, 3]
        s_in = sb("s_in", [P, RING, NB])
        s_row = sb("s_row", [12, RING, ROWS], BF16)
        gather_now = sb("gather_now", [P, RING, 2 * EB], I32)
        late_now = sb("late_now", [P, EB], I32)
        late_none = sb("late_none", [1, 1 + EB, F])
        late_row = sb("late_row", [P, EB * F])
        s_all = sb("s_all", [S_ROWS, S_COLS])
        s_rest = sb("s_rest", [S_ROWS, 2, S_COLS])
        s_terms = sb("s_terms", [S_ROWS, 3, S_COLS], BF16)
        scatter_now = sb("scatter_now", [P, RING, EB], I32)
        g_in = sb("g_in", [P, RING, 2 * EB, F + 1])
        hg_row = sb("hg_row", [P, RING, 2 * EB, F])
        hg_col = sb("hg_col", [P, RING, 2 * EB, P])
        xh_dst = sb("xh_dst", [P, RING, EB, F])
        flags = sb("flags", [P, RING, 3, EW], BF16)
        rdeg = sb("rdeg", [P, RING, EW])
        e_in = sb("e_in", [ED + 1, RING, EW])
        gain = sb("gain", [P, RING, 3, EB])
        seg_sum = sb("seg_sum", [P, RING, EW])
        seg_agg = sb("seg_agg", [P, RING, 3, EW])
        comb = sb("comb", [P, 3, EB, F])
        y_edge = sb("y_edge", [P, RING, EB, F])
        NS = NB + 2 * EB
        stats = sb("stats", [P, RING, NS, 6])
        mean2 = sb("mean2", [P, RING, NS])
        mdiff = sb("mdiff", [P, 3, NS])
        var = sb("var", [P, RING, NS])
        std = sb("std", [P, RING, NS])
        rstd = sb("rstd", [P, RING, NS])
        nmean = sb("nmean", [P, RING, NS])

        flat = work[:, :, :, :, :].rearrange("p a r n f -> p (a r n f)")
        places = [0]

        def place(width):
            places[0] += width
            return flat[:, places[0] - width:places[0]]

        all_dst = place(EPAD)
        edge_rows = place(ET * (ED + 2)).rearrange("p (t c) -> p t c", c=ED + 2)
        less = place(EPAD // 8).bitcast(BF16)
        equal = place(P)
        earlier = place(P)
        dst_key = place(ET)
        rank_f = place(ET)
        unsorted = sb("unsorted", [ET, 2])
        unsorted_i = sb("unsorted_i", [1, 1], I32)
        order_x = sb("order_x", [ET, P])
        counts = sb("counts", [P, 5])
        rank_i = sb("rank_i", [P, ET], I32)
        rank_now = sb("rank_now", [P, 1], I32)
        edge_now = sb("edge_now", [P, ED + 2])
        ends = sb("ends", [1, ED + 2])
        dst_f = sb("dst_f", [ET, 3, P])
        cols_f = sb("cols_f", [P, 3, ET])

        turn_e = ps("turn_e", [P, 4, P])
        turn_d = ps("turn_d", [P, NB, P])
        msg_ps = ps("msg_ps", [P, 512])
        post_d = ps("post_d", [P, NB, F])
        post_e = ps("post_e", [P, EB, 4, F])

        weights_in = sem("weights_in")
        lists_in = sem("lists_in")
        set_pool = sem("set_pool")
        set_dve = sem("set_dve")
        set_act = sem("set_act")
        set_pe = sem("set_pe")
        pool_waited = sem("pool_waited")
        heads_ready, carry_ready = sem("heads_ready"), sem("carry_ready")
        gather_lists_ready, lists_ready, degree_ready = sem("gather_lists_ready"), sem("lists_ready"), sem("degree_ready")
        rows_ready, scalers_ready = sem("rows_ready"), sem("scalers_ready")
        parts_ready, set_ready = sem("parts_ready"), sem("set_ready")
        spread_out = sem("spread_out")
        e_copied = sem("e_copied")
        order_ready, order_known = sem("order_ready"), sem("order_known")
        s_all_in, s_split, s_spread = sem("s_all_in"), sem("s_split"), sem("s_spread")
        sort_pool, sort_dve = sem("sort_pool"), sem("sort_dve")
        sort_loaded = sem("sort_loaded")
        rank_step = sem("rank_step")
        ranked = sem("ranked")
        row_copied, row_scattered = sem("row_copied"), sem("row_scattered")
        relisted = sem("relisted")
        parts_in = sem("parts_in")
        x_loaded, s_loaded, g_loaded = sems("x_loaded"), sems("s_loaded"), sems("g_loaded")
        edge_loaded, s_row_loaded = sems("edge_loaded"), sems("s_row_loaded")
        y_stored, y_scattered = sems("y_stored"), sems("y_scattered")
        late_copied, late_loaded, late_scattered = sem("late_copied"), sem("late_loaded"), sem("late_scattered")
        index_ready, scatter_index_ready = sem("index_ready"), sem("scatter_index_ready")
        mean_step = sem("mean_step")
        var_ready = sem("var_ready")
        std_ready = sem("std_ready")
        rstd_ready = sem("rstd_ready")
        norm_ready = sem("norm_ready")
        h_ready = sem("h_ready")
        xh_ready = sem("xh_ready")
        xh_dst_ready = sem("xh_dst_ready")
        gain_ready = sem("gain_ready")
        turned_e, turned_d = sem("turned_e"), sem("turned_d")
        col_e_ready, col_d_ready = sem("col_e_ready"), sem("col_d_ready")
        msg_ready = sem("msg_ready")
        scanned = sem("scanned")
        agg_ready = sem("agg_ready")
        mm_d_ready = sem("mm_d_ready")
        scaled = sem("scaled")
        post_d_ready = sem("post_d_ready")
        post_e_ready = sem("post_e_ready")
        comb_step = sem("comb_step")
        y_edge_ready = sem("y_edge_ready")
        y_out_ready = sem("y_out_ready")
        dense_stored = sem("dense_stored")

        WEIGHTS = 16 * 9
        LISTS = 16 * 6

        def row0(step, lag):
            if not step.looped:
                return min(step.at(lag) * ROWS, LAST_ROW0)
            return step.at(lag) * ROWS

        block = ctx.enter_context(nc.Block())

        @block.sync
        def _(sp):
            sp.dma_start(s_all[:, :], snorm.rearrange("(p c) a -> p (c a)", c=S_COLS)).then_inc(s_all_in, 16)
            sp.dma_start(dst_i[:, 0, :], dst_ext[0:EPAD].rearrange("(t p) -> t p", p=P)).then_inc(lists_in, 16)
            sp.dma_start(dst_i[:, 1, :], dst_ext[1:EPAD + 1].rearrange("(t p) -> t p", p=P)).then_inc(lists_in, 16)
            sp.dma_start(dst_i[:, 2, :], dst_ext[2:EPAD + 2].rearrange("(t p) -> t p", p=P)).then_inc(lists_in, 16)
            def body(t):
                if not t.looped and t.c == RING:
                    sp.wait_ge(parts_ready, 1)
                    sp.dma_start(bias3[:, :], parts_1[0:1, 0, :, :]).then_inc(parts_in, 16)
                    for r in range(3):
                        sp.dma_start(add12[3 * r:3 * r + 3, :], parts_1[0:1, 0, r:r + 1, :].broadcast_to((1, 3, F))).then_inc(parts_in, 16)
                    sp.dma_start(add12[9:12, :], parts_1[0:1, 1, :, :]).then_inc(parts_in, 16)
                if t.has(0):
                    k = t.slot(0)
                    if t.reused(0):
                        sp.wait_ge(rows_ready, 1)
                        sp.wait_ge(xh_ready, t.at(0) - RING + 1)
                    sp.dma_start(x_in[:, k, :, :],
                                 x[bass.ds(row0(t, 0), ROWS), :].rearrange("(p r) f -> p r f", p=P)
                                 ).then_inc(x_loaded[k], 16)
                if t.has(NORM):
                    k = t.slot(NORM)
                    if t.reused(NORM):
                        sp.wait_ge(rows_ready, 1)
                        sp.wait_ge(post_d_ready, t.at(NORM) - RING + 1)
                        sp.wait_ge(agg_ready, t.at(NORM) - RING + 1)
                    elif t.c == NORM:
                        sp.wait_ge(spread_out, 32)
                        sp.wait_ge(e_copied, 16)
                        sp.wait_ge(s_spread, 48)
                    sp.dma_start(s_in[:, k, :],
                                 snorm[bass.ds(row0(t, NORM), ROWS), :].rearrange("(p r) a -> p (r a)", p=P)
                                 ).then_inc(s_loaded[k], 16)
                    sp.dma_start(s_row[0:9, k, :],
                                 s_dram.rearrange("r k n -> (r k) n")[:, bass.ds(row0(t, NORM), ROWS)]
                                 ).then_inc(s_row_loaded[k], 16)
                    e0 = t.at(NORM) * EW
                    sp.dma_start(flags[:, k, :, :],
                                 flags_dram[:, bass.ds(e0, EW)].partition_broadcast(P)).then_inc(edge_loaded[k], 16)
                    sp.dma_start(rdeg[:, k, :],
                                 rdeg_dram[:, bass.ds(e0, EW)].partition_broadcast(P)).then_inc(edge_loaded[k], 16)
                    sp.dma_start(e_in[0:ED, k, :], e_dram[:, bass.ds(e0, EW)]).then_inc(edge_loaded[k], 16)
                if t.has(CONFIRM):
                    sp.wait_ge(rows_ready, 1)
                    sp.wait_ge(y_stored[t.slot(CONFIRM)], 16 * (t.lap(CONFIRM) + 1))
                    sp.sem_inc(dense_stored, 1)
                if t.has(POST):
                    k = t.slot(POST)
                    sp.wait_ge(y_out_ready, t.at(POST) + 1)
                    if not t.looped and t.c - POST == STEPS - 1:
                        sp.wait_ge(y_stored[(k - 1) % RING], 16 * (t.lap(POST + 1) + 1))
                    sp.dma_start(out[bass.ds(row0(t, POST), ROWS), :].rearrange("(p r) f -> p r f", p=P),
                                 y_out[:, k, :, :]).then_inc(y_stored[k], 16)

            run_steps(sp, 0, CONFIRM, body)

        def scatter_late(pool):
            with pool.Fori(0, STEPS) as j:
                with pool.If(pool.value_load(late_i[0:1, bass.ds(j, 1)], min_val=0, max_val=1) > 0):
                    pool.tensor_copy(late_now[:, :], index[:, bass.ds(j, 1), 2 * EB:3 * EB].rearrange("p a c -> p (a c)")
                                     ).then_inc(late_copied, 1)
                    pool.dma_start(late_row[:, :], late_dram[bass.ds(j, 1), :, :].rearrange("a p f -> (a p) f")
                                   ).then_inc(late_loaded, 16)
                    pool.wait_ge(late_copied, j + 1)
                    pool.wait_ge(late_loaded, j * 16 + 16)
                    pool.sem_inc(pool_waited, 1)
                    for c in range(EB):
                        pool.indirect_dma_start(out, bass.IndirectOffsetOnAxis(late_now[:, c:c + 1], 0),
                                                late_row[:, c * F:(c + 1) * F], None, bounds_check=N - 1, oob_is_err=False,
                                                ).then_inc(late_scattered, 16)
                with pool.Else():
                    pool.sem_inc(late_copied, 1)
                    pool.dma_start(late_none[:, 0, :], beta.rearrange("(a f) -> a f", a=1)).then_inc(late_loaded, 16)
                    for c in range(EB):
                        pool.dma_start(late_none[:, 1 + c, :], beta.rearrange("(a f) -> a f", a=1)
                                       ).then_inc(late_scattered, 16)
                    pool.wait_ge(late_loaded, j * 16 + 16)
                pool.wait_ge(late_scattered, j * (16 * EB) + 16 * EB)

        SORT_LOADS = 16 * 3
        RELISTS = 16 * (6 + ED)

        def put_in_order(pool):
            pool.memset(edge_rows[:, :, :], 0.0).then_inc(sort_pool, 1)
            pool.memset(ends[:, :], -1.0).then_inc(sort_pool, 1)
            pool.memset(earlier[:, :], 1.0).then_inc(sort_pool, 1)
            pool.wait_ge(sort_pool, 3)
            pool.affine_select(out=earlier[:, :], in_=earlier[:, :], compare_op=ALU.is_gt, fill=0.0,
                               base=0, pattern=[[-1, P]], channel_multiplier=1).then_inc(sort_pool, 1)
            pool.dma_start(all_dst.bitcast(I32), dst_ext[1:EPAD + 1].rearrange("(a e) -> a e", a=1).partition_broadcast(P)
                           ).then_inc(sort_loaded, 16)
            full = E // P
            pool.dma_start(edge_rows[:, 0:full, 0:ED], e_row[0:full * P, :].rearrange("(t p) c -> p t c", p=P)
                           ).then_inc(sort_loaded, 16)
            pool.dma_start(edge_rows[0:E - full * P, full, 0:ED], e_row[full * P:E, :]).then_inc(sort_loaded, 16)
            pool.dma_start(sorted_dram[0:1, :], ends[:, :]).then_inc(row_scattered, 16)
            pool.dma_start(sorted_dram[EPAD + 1:EPAD + 2, :], ends[:, :]).then_inc(row_scattered, 16)
            pool.wait_ge(ranked, 1)
            with pool.Fori(0, ET) as t:
                pool.tensor_copy(rank_now[:, :], rank_i[:, bass.ds(t, 1)]).then_inc(row_copied, 1)
                pool.tensor_copy(edge_now[:, :], edge_rows[:, bass.ds(t, 1), :].rearrange("p a c -> p (a c)")
                                 ).then_inc(row_copied, 1)
                pool.wait_ge(row_copied, t * 2 + 2)
                pool.sem_inc(pool_waited, 1)
                pool.indirect_dma_start(sorted_dram, bass.IndirectOffsetOnAxis(rank_now[:, 0:1], 0),
                                        edge_now[:, :], None).then_inc(row_scattered, 16)
                pool.wait_ge(row_scattered, t * 16 + 48)
            pool.wait_ge(e_copied, 16)
            for shift in range(3):
                rows = sorted_dram[shift:shift + EPAD, ED:ED + 1]
                pool.dma_start(dst_f[:, shift, :], rows.rearrange("(t p) c -> t (p c)", p=P),
                               allow_slow_non_contiguous=True).then_inc(relisted, 16)
            for col, (shift, what) in enumerate([(1, ED + 1), (1, ED), (2, ED)]):
                rows = sorted_dram[shift:shift + EPAD, what:what + 1]
                pool.dma_start(cols_f[:, col, :], rows.rearrange("(t p) c -> p (t c)", p=P),
                               allow_slow_non_contiguous=True).then_inc(relisted, 16)
            for c in range(ED):
                pool.dma_start(e_dram[c:c + 1, :].rearrange("a (t p) -> (a t) p", p=P),
                               sorted_dram[1:EPAD + 1, c:c + 1].rearrange("(t p) c -> t (p c)", p=P),
                               allow_slow_non_contiguous=True).then_inc(relisted, 16)

        @block.gpsimd
        def _(pool):
            pool.memset(ident[:, :], 0.0).then_inc(set_pool, 1)
            pool.wait_ge(set_pool, 1)
            pool.affine_select(out=ident[:, :], in_=ident[:, :], compare_op=ALU.not_equal, fill=1.0,
                               base=0, pattern=[[-1, P]], channel_multiplier=1).then_inc(set_pool, 1)
            pool.memset(e_in[:, :, :], 1.0).then_inc(set_pool, 1)
            pool.memset(s_row[:, :, :], 1.0).then_inc(set_pool, 1)
            pool.iota(edge_i[:, :], pattern=[[1, P]], base=0, channel_multiplier=P).then_inc(set_pool, 1)
            pool.wait_ge(order_known, 1)
            with pool.If(pool.value_load(unsorted_i[0:1, 0:1], min_val=0, max_val=1) > 0):
                put_in_order(pool)
            with pool.Else():
                pool.sem_inc(sort_pool, 1)
            pool.wait_ge(gather_lists_ready, 1)

            def body(t):
                if t.has(0):
                    k = t.slot(0)
                    if t.reused(0):
                        pool.wait_ge(xh_dst_ready, t.at(0) - RING + 1)
                        pool.wait_ge(xh_ready, t.at(0) - RING + 1)
                    pool.tensor_copy(gather_now[:, k, :], index[:, bass.ds(t.at(0), 1), 0:2 * EB].rearrange("p a c -> p (a c)")
                                     ).then_inc(index_ready, 1)
                    pool.wait_ge(index_ready, t.at(0) + 1)
                    pool.sem_inc(pool_waited, 1)
                    for c in range(2 * EB):
                        pool.indirect_dma_start(g_in[:, k, c, :], None, x_s,
                                                bass.IndirectOffsetOnAxis(gather_now[:, k, c:c + 1], 0),
                                                ).then_inc(g_loaded[k], 16)
                if t.has(TURN):
                    k = t.slot(TURN)
                    pool.wait_ge(h_ready, t.at(TURN) + 1)
                    if t.reused(TURN):
                        pool.wait_ge(y_out_ready, t.at(TURN) - RING + 1)
                    pool.tensor_tensor(xh[:, k, :, :], x_in[:, k, :, :], h_row[:, k, :, :], ALU.add).then_inc(xh_ready, 1)
                if t.has(SCATTER):
                    k = t.slot(SCATTER)
                    if not t.after(SCATTER):
                        pool.wait_ge(lists_ready, 1)
                    if t.reused(SCATTER):
                        pool.wait_ge(y_scattered[k], 32 * t.lap(SCATTER))
                    pool.tensor_copy(scatter_now[:, k, :], index[:, bass.ds(t.at(SCATTER), 1), 2 * EB:3 * EB].rearrange("p a c -> p (a c)")
                                     ).then_inc(scatter_index_ready, 1)
                    late = pool.value_load(late_i[0:1, bass.ds(t.at(SCATTER), 1)], min_val=0, max_val=1)
                    pool.wait_ge(scatter_index_ready, t.at(SCATTER) + 1)
                    pool.wait_ge(y_edge_ready, t.at(SCATTER) + 1)
                    pool.wait_ge(dense_stored, t.at(SCATTER) + AHEAD if t.looped else min(t.at(SCATTER) + AHEAD, STEPS))
                    pool.sem_inc(pool_waited, 1)
                    with pool.If(late > 0):
                        for c in range(EB):
                            pool.dma_start(late_dram[bass.ds(t.at(SCATTER), 1), :, c * F:(c + 1) * F].rearrange("a p f -> (a p) f"),
                                           y_edge[:, k, c, :]).then_inc(y_scattered[k], 16)
                    with pool.Else():
                        for c in range(EB):
                            pool.indirect_dma_start(out, bass.IndirectOffsetOnAxis(scatter_now[:, k, c:c + 1], 0),
                                                    y_edge[:, k, c, :], None, bounds_check=N - 1, oob_is_err=False,
                                                    ).then_inc(y_scattered[k], 16)

            run_steps(pool, 0, SCATTER, body)
            for k in range(RING):
                pool.wait_ge(y_scattered[k], 32 * len(range(k, STEPS, RING)))
            pool.wait_ge(dense_stored, STEPS)
            with pool.If(pool.value_load(late_i[0:1, STEPS:STEPS + 1], min_val=0, max_val=1) > 0):
                scatter_late(pool)
            with pool.Else():
                pool.sem_inc(pool_waited, 1)

        @block.tensor
        def _(pe):
            pe.wait_ge(set_pool, 2)
            pe.wait_ge(order_ready, 1)
            pe.transpose(turn_e[0:1, 0, 0:ET], unsorted[:, 0:1], ident[0:ET, 0:ET]).then_inc(set_pe, 1)
            pe.wait_ge(heads_ready, 1)
            pe.transpose(msg_ps[0:1, 0:ET], heads[:, 0:1], ident[0:ET, 0:ET])
            pe.transpose(msg_ps[0:1, P:P + ET], heads[:, 1:2], ident[0:ET, 0:ET]).then_inc(set_pe, 1)
            pe.wait_ge(carry_ready, 1)
            pe.transpose(msg_ps[0:ET, 2 * P:2 * P + 1], carry[0:1, 0:ET], ident[0:1, 0:1]).then_inc(set_pe, 1)
            pe.wait_ge(scalers_ready, 1)
            pe.transpose(msg_ps[:, 0:ET], scaler[:, 1, :], ident[0:ET, 0:ET])
            pe.transpose(msg_ps[:, P:P + ET], scaler[:, 2, :], ident[0:ET, 0:ET]).then_inc(set_pe, 1)

            def body(t):
                if not t.after(POST) and t.has(POST):
                    pe.wait_ge(parts_in, 16 * 5)
                if t.has(POST):
                    k = t.slot(POST)
                    pe.wait_ge(agg_ready, t.at(POST) + 1)
                    if t.after(POST):
                        pe.wait_ge(comb_step, 3 * t.at(POST))
                    for c in range(EB):
                        pe.matmul(post_e[:, c, 0, :], ones3[:, :], bias3[:, :], start=True, stop=False,
                                  skip_group_check=True)
                        pe.matmul(post_e[:, c, 0, :], hg_col[:, k, EB + c, :], w_h[:, :], start=False, stop=False,
                                  skip_group_check=True)
                        for a in range(3):
                            last = pe.matmul(post_e[:, c, 0:3, :], seg_agg[:, k, a, c * P:(c + 1) * P], w_agg[:, a, :, :],
                                             start=False, stop=(a == 2), skip_group_check=True)
                        if c == 0:
                            pe.wait_ge(s_row_loaded[k], 16 * (t.lap(POST) + 1))
                            pe.wait_ge(scaled, t.at(POST) + 1)
                            for j in range(NB):
                                rows = s_row[:, k, :].rearrange("a (p r) -> a r p", r=NB)[:, j, :]
                                added = pe.matmul(post_d[:, j, :], rows, add12[:, :],
                                                  start=False, stop=(j % 4 == 3), skip_group_check=True)
                            added.then_inc(post_d_ready, 1)
                    last.then_inc(post_e_ready, 1)
                if not t.after(MSG) and t.has(MSG):
                    pe.wait_ge(set_ready, 1)
                    pe.wait_ge(weights_in, WEIGHTS)
                if t.has(MSG):
                    k = t.slot(MSG)
                    pe.wait_ge(col_e_ready, t.at(MSG) + 1)
                    pe.wait_ge(edge_loaded[k], 48 * (t.lap(MSG) + 1))
                    if t.after(MSG):
                        pe.wait_ge(agg_ready, t.at(MSG))
                    pe.matmul(msg_ps[:, 0:EW], w_msg[:, 0, :], hg_col[:, k, 0:EB, :], start=True, stop=False)
                    pe.matmul(msg_ps[:, 0:EW], w_msg[:, 1, :], hg_col[:, k, EB:2 * EB, :], start=False, stop=False)
                    pe.matmul(msg_ps[:, 0:EW], w_edge[:, :], e_in[:, k, :], start=False, stop=True
                              ).then_inc(msg_ready, 1)
                    pe.wait_ge(col_d_ready, t.at(MSG) + 1)
                    if t.after(MSG):
                        pe.wait_ge(y_out_ready, t.at(MSG))
                    for j in range(NB):
                        last = pe.matmul(post_d[:, j, :], h_col[:, k, j, :], w_h[:, :],
                                         start=(j % 4 == 0), stop=False, skip_group_check=True)
                    last.then_inc(mm_d_ready, 1)
                if t.has(TURN):
                    k = t.slot(TURN)
                    pe.wait_ge(h_ready, t.at(TURN) + 1)
                    if t.after(TURN):
                        pe.wait_ge(col_e_ready, t.at(TURN))
                        pe.wait_ge(col_d_ready, t.at(TURN))
                    for c in range(2 * EB):
                        last = pe.transpose(turn_e[:, c, :], hg_row[:, k, c, :], ident[:, :])
                    last.then_inc(turned_e, 1)
                    for j in range(NB):
                        last = pe.transpose(turn_d[:, j, :], h_row[:, k, j, :], ident[:, :])
                    last.then_inc(turned_d, 1)

            run_steps(pe, TURN, POST, body)

        @block.scalar
        def _(act):
            act.dma_start(cols_i[:, 0, :], src_col).then_inc(lists_in, 16)
            act.dma_start(cols_i[:, 1, :], dst_col).then_inc(lists_in, 16)
            act.dma_start(cols_i[:, 2, :], next_col).then_inc(lists_in, 16)
            act.dma_start(gamma_b[:, :], gamma.rearrange("(a f) -> a f", a=1).partition_broadcast(P)).then_inc(weights_in, 16)
            act.dma_start(w_raw[:, :, :], w_post.rearrange("(b k) f -> k b f", k=P)).then_inc(weights_in, 16)
            act.dma_start(beta_b[:, :], beta.rearrange("(a f) -> a f", a=1).partition_broadcast(P)).then_inc(weights_in, 16)
            act.dma_start(b_post_1[:, :], b_post.rearrange("(a f) -> a f", a=1)).then_inc(weights_in, 16)
            act.dma_start(beta_1[:, :], beta.rearrange("(a f) -> a f", a=1)).then_inc(weights_in, 16)
            act.dma_start(w_msg[:, 0, :], w_pre[0:P, :]).then_inc(weights_in, 16)
            act.dma_start(w_msg[:, 1, :], w_pre[P:2 * P, :]).then_inc(weights_in, 16)
            act.dma_start(w_edge[0:ED, :], w_pre[2 * P:2 * P + ED, :]).then_inc(weights_in, 16)
            act.dma_start(w_edge[ED:ED + 1, :], b_pre.rearrange("(a f) -> a f", a=1)).then_inc(weights_in, 16)
            act.dma_start(e_dram, e_t).then_inc(e_copied, 16)

            act.wait_ge(s_split, 5)
            for r in range(3):
                act.dma_start(s_dram[r].rearrange("k (p c) -> p k c", c=S_COLS), s_terms[:, :, :]).then_inc(s_spread, 16)
            act.wait_ge(degree_ready, 1)
            nc.scalar.activation(scaler[:, 0, :], degree[:, 0, :], ACT.Ln, bias=two_c[0:ET, 0:1]).then_inc(set_act, 1)
            nc.scalar.activation(sqrt_table[:, :], two_c[:, :], ACT.Sqrt).then_inc(set_act, 1)
            act.wait_ge(rows_ready, 1)
            act.dma_start(flags_dram.rearrange("c (t p) -> t c p", p=P), flag_row[:, :, :]).then_inc(spread_out, 16)
            act.dma_start(rdeg_dram.rearrange("a (t p) -> (a t) p", p=P), rdeg_row[:, :]).then_inc(spread_out, 16)

            def body(t):
                if t.has(MSG):
                    k = t.slot(MSG)
                    act.wait_ge(turned_e, t.at(MSG) + 1)
                    nc.scalar.activation(hg_col[:, k, :, :], turn_e[:, :, :], ACT.Copy).then_inc(col_e_ready, 1)
                if t.has(POST):
                    k = t.slot(POST)
                    act.wait_ge(s_loaded[k], 16 * (t.lap(POST) + 1))
                    act.wait_ge(mm_d_ready, t.at(POST) + 1)
                    for j in range(NB):
                        last = nc.scalar.activation(post_d[:, j, :], post_d[:, j, :], ACT.Copy, scale=s_in[:, k, j:j + 1])
                    last.then_inc(scaled, 1)
                if t.has(NORM):
                    k = t.slot(NORM)
                    act.wait_ge(var_ready, t.at(NORM) + 1)
                    nc.scalar.activation(std[:, k, :], var[:, k, :], ACT.Sqrt, bias=eps_c[:, 0:1], scale=1.0 / F
                                         ).then_inc(std_ready, 1)
                if t.has(MSG):
                    k = t.slot(MSG)
                    act.wait_ge(turned_d, t.at(MSG) + 1)
                    for b in range(NB // 4):
                        last = nc.scalar.activation(h_col[:, k, 4 * b:4 * b + 4, :], turn_d[:, 4 * b:4 * b + 4, :], ACT.Copy)
                    last.then_inc(col_d_ready, 1)
                if t.has(NORM):
                    k = t.slot(NORM)
                    act.wait_ge(norm_ready, t.at(NORM) + 1)
                    if t.reused(NORM):
                        act.wait_ge(xh_dst_ready, t.at(NORM) - RING + 1)
                        act.wait_ge(xh_ready, t.at(NORM) - RING + 1)
                        act.wait_ge(turned_d, t.at(NORM) - RING + 1)
                    for c in range(2 * EB):
                        nc.scalar.activation(hg_row[:, k, c, :], g_in[:, k, c, 0:F], ACT.Relu,
                                             bias=nmean[:, k, NB + c:NB + c + 1], scale=rstd[:, k, NB + c:NB + c + 1])
                    for j in range(NB):
                        last = nc.scalar.activation(h_row[:, k, j, :], x_in[:, k, j, :], ACT.Relu,
                                                    bias=nmean[:, k, j:j + 1], scale=rstd[:, k, j:j + 1])
                    last.then_inc(h_ready, 1)

            run_steps(act, NORM, POST, body)

        def rank_edges(dve):
            dve.wait_ge(sort_loaded, SORT_LOADS)
            dve.wait_ge(sort_pool, 4)
            dve.tensor_copy(all_dst, all_dst.bitcast(I32)).then_inc(sort_dve, 1)
            dve.tensor_copy(dst_key, cols_i[:, 1, :]).then_inc(sort_dve, 1)
            dve.tensor_copy(edge_rows[:, :, ED], cols_i[:, 1, :]).then_inc(sort_dve, 1)
            dve.tensor_copy(edge_rows[:, :, ED + 1], cols_i[:, 0, :]).then_inc(sort_dve, 1)
            dve.wait_ge(sort_dve, 4)
            quarter = EPAD // 4
            with dve.Fori(0, ET) as t:
                key = dst_key[:, bass.ds(t, 1)]
                tile = all_dst[:, bass.ds(t * P, P)]
                for c in range(4):
                    dve.tensor_scalar(less, all_dst[:, c * quarter:(c + 1) * quarter], key, None, ALU.is_lt, ALU.add,
                                      accum_out=counts[:, c:c + 1]).then_inc(rank_step, 1)
                    dve.wait_ge(rank_step, t * 7 + (c + 1))
                dve.scalar_tensor_tensor(out=equal, in0=tile, scalar=key, in1=earlier, op0=ALU.is_equal, op1=ALU.mult,
                                         accum_out=counts[:, 4:5]).then_inc(rank_step, 1)
                dve.wait_ge(rank_step, t * 7 + 5)
                dve.tensor_reduce(rank_f[:, bass.ds(t, 1)], counts[:, :], AX_X, ALU.add).then_inc(rank_step, 1)
                dve.tensor_scalar(tile, tile, -0.5, None, ALU.add).then_inc(rank_step, 1)
                dve.wait_ge(rank_step, t * 7 + 7)
            dve.tensor_scalar(rank_i[:, :], rank_f, 1.0, None, ALU.add).then_inc(ranked, 1)
            dve.wait_ge(relisted, RELISTS)
            dve.tensor_copy(dst_i[:, :, :], dst_f[:, :, :]).then_inc(sort_dve, 1)
            dve.tensor_copy(cols_i[:, :, :], cols_f[:, :, :]).then_inc(sort_dve, 1)
            dve.wait_ge(sort_dve, 6)

        @block.vector
        def _(dve):
            done = [0]

            def then(ins):
                done[0] += 1
                return ins.then_inc(set_dve, 1)

            def chain(ins):
                then(ins)
                dve.wait_ge(set_dve, done[0])

            def mark(reached):
                dve.wait_ge(set_dve, done[0])
                dve.sem_inc(reached, 1)

            then(dve.memset(ones3[:, :], 1.0))
            then(dve.memset(eps_c[:, :], LN_EPS))
            then(dve.memset(two_c[:, :], 2.0))
            then(dve.memset(seg_sum[:, RING - 1, EW - 1:EW], 0.0))
            then(dve.memset(seg_agg[:, RING - 1, :, EW - 1:EW], 0.0))
            chain(dve.memset(carry[:, :], 0.0))
            dve.wait_ge(s_all_in, 16)
            left = s_all[:, :]
            for k in range(3):
                dve.tensor_copy(s_terms[:, k, :], left).then_inc(s_split, 1)
                if k < 2:
                    dve.wait_ge(s_split, 2 * k + 1)
                    dve.tensor_tensor(s_rest[:, k, :], left, s_terms[:, k, :], ALU.subtract).then_inc(s_split, 1)
                    dve.wait_ge(s_split, 2 * k + 2)
                    left = s_rest[:, k, :]
            dve.wait_ge(lists_in, LISTS)
            chain(dve.tensor_tensor(order_x[:, :], dst_i[:, 0, :], dst_i[:, 1, :], ALU.is_gt))
            chain(dve.tensor_reduce(unsorted[:, 0:1], order_x[:, :], AX_X, ALU.max))
            mark(order_ready)
            dve.wait_ge(set_pe, 1)
            chain(dve.tensor_reduce(unsorted_i[:, :], turn_e[0:1, 0, 0:ET], AX_X, ALU.max))
            mark(order_known)
            with dve.If(dve.value_load(unsorted_i[0:1, 0:1], min_val=0, max_val=1) > 0):
                rank_edges(dve)
            with dve.Else():
                dve.sem_inc(sort_dve, 1)
            def pairs(a):
                return a.rearrange("p (j c) -> p j c", c=EB)
            then(dve.tensor_copy(index[:, :, 0:EB], pairs(cols_i[:, 0, :])))
            then(dve.tensor_scalar(index[:, :, EB:2 * EB], pairs(cols_i[:, 1, :]), float(N - 1), None, ALU.min))
            mark(gather_lists_ready)
            chain(dve.tensor_tensor(flag_f[:, :], dst_i[:, 0, :], dst_i[:, 1, :], ALU.is_equal))
            then(dve.tensor_copy(flag_row[:, 0, :], flag_f[:, :]))
            chain(dve.tensor_scalar(flag_n[:, :], flag_f[:, :], -1.0, BIG, ALU.add, ALU.mult))
            chain(dve.scalar_tensor_tensor(out=local[:, :], in0=flag_f[:, :], scalar=BIG, in1=flag_n[:, :],
                                           op0=ALU.mult, op1=ALU.add))
            then(dve.tensor_copy(flag_row[:, 1, :], local[:, :]))
            chain(dve.tensor_scalar(flag_row[:, 2, :], local[:, :], -1.0, None, ALU.mult))
            dve.wait_ge(set_pool, 5)
            chain(dve.scalar_tensor_tensor(out=flag_n[:, :], in0=flag_f[:, :], scalar=1.0, in1=edge_i[:, :],
                                           op0=ALU.is_lt, op1=ALU.mult))
            chain(dve.tensor_tensor_scan(local[:, :], flag_n[:, :], flag_n[:, :], 0.0, ALU.max, ALU.max))
            then(dve.tensor_copy(heads[:, 0:1], local[:, P - 1:P]))
            chain(dve.tensor_reduce(heads[:, 1:2], dst_i[:, 1, :], AX_X, ALU.max))
            mark(heads_ready)
            dve.wait_ge(set_pe, 2)
            chain(dve.tensor_copy(heads_t[:, :, :], msg_ps[0:1, 0:2 * P].rearrange("a (b t) -> a b t", b=2)[:, :, 0:ET]))
            chain(dve.tensor_tensor_scan(carry[0:1, 1:ET + 1], heads_t[:, 0, :], heads_t[:, 0, :], 0.0, ALU.max, ALU.max))
            mark(carry_ready)
            dve.wait_ge(set_pe, 3)
            chain(dve.tensor_scalar(cand[:, :], local[:, :], msg_ps[0:ET, 2 * P:2 * P + 1], None, ALU.max))
            chain(dve.tensor_tensor(degree[:, 0, :], edge_i[:, :], cand[:, :], ALU.subtract))
            mark(degree_ready)
            chain(dve.tensor_scalar(degree[:, 1, :], degree[:, 0, :], 1.0, None, ALU.add))
            chain(dve.reciprocal(rdeg_row[:, :], degree[:, 1, :]))
            mark(rows_ready)
            def scale_weights():
                dve.wait_ge(set_act, 1)
                then(dve.tensor_scalar(scaler[:, 1, :], scaler[:, 0, :], 1.0 / AVG_D_LOG, None, ALU.mult))
                chain(dve.reciprocal(cand[:, :], scaler[:, 0, :]))
                chain(dve.tensor_scalar(scaler[:, 2, :], cand[:, :], AVG_D_LOG, None, ALU.mult))
                mark(scalers_ready)
                dve.wait_ge(weights_in, WEIGHTS)
                chain(dve.tensor_scalar(scale_b[:, :], gamma_b[:, :], 1.0 / math.sqrt(1.0 + BN_EPS), None, ALU.mult))
                then(dve.tensor_tensor(w_h[:, :], w_raw[:, 0, :], scale_b[:, :], ALU.mult))
                dve.wait_ge(set_pe, 4)
                chain(dve.tensor_copy(amp_att[:, :, :], msg_ps[:, 0:2 * P].rearrange("p (b t) -> p b t", b=2)[:, :, 0:ET]))
                mark(set_ready)

            def scale_rest():
                w_post_agg = w_raw[:, 1:10, :].rearrange("p (c a) f -> p c a f", a=3)
                then(dve.tensor_tensor(w_agg[:, :, :, :].rearrange("p a c f -> p c a f"), w_post_agg,
                                       scale_b[:, :].rearrange("p (a c f) -> p a c f", a=1, c=1).broadcast_to((P, 3, 3, F)),
                                       ALU.mult))
                then(dve.tensor_tensor(bias_1[:, 0, :], b_post_1[:, :], scale_b[0:1, :], ALU.mult))
                chain(dve.tensor_copy(bias_1[:, 1, :], beta_1[:, :]))
                src = bias_1[:, :, :]
                for k in range(3):
                    chain(dve.tensor_copy(parts_1[:, :, k, :], src))
                    if k < 2:
                        chain(dve.tensor_tensor(rest_1[:, k, :, :], src, parts_1[:, :, k, :], ALU.subtract))
                        src = rest_1[:, k, :, :]
                mark(parts_ready)

            def list_scatters():
                chain(dve.tensor_tensor(same_next[:, :], cols_i[:, 1, :], cols_i[:, 2, :], ALU.is_equal))
                then(dve.scalar_tensor_tensor(out=index[:, :, 2 * EB:3 * EB], in0=pairs(same_next[:, :]), scalar=float(SKIP),
                                              in1=pairs(cols_i[:, 1, :]), op0=ALU.mult, op1=ALU.add))
                chain(dve.tensor_reduce(top_dst[:, :], heads_t[:, 1, :].rearrange("a (j c) -> a j c", c=EB), AX_X, ALU.max))
                chain(dve.tensor_scalar(need_i[:, 0, :], top_dst[:, :], float(N - 1), float(STEPS * ROWS - N + ROWS),
                                        ALU.min, ALU.add))
                chain(dve.tensor_scalar(need_i[:, 1, :], need_i[:, 0, :], GROUP_SHIFT, None, ALU.logical_shift_right))
                chain(dve.scalar_tensor_tensor(out=late_f[:, 0:STEPS], in0=need_i[:, 1, :], scalar=-float(AHEAD),
                                               in1=edge_i[0:1, 0:STEPS], op0=ALU.add, op1=ALU.is_gt))
                chain(dve.tensor_reduce(late_f[:, STEPS:STEPS + 1], late_f[:, 0:STEPS], AX_X, ALU.max))
                then(dve.tensor_copy(late_i[:, :], late_f[:, :]))
                mark(lists_ready)

            def combine(t, a):
                k = t.slot(POST)
                for c in range(EB):
                    last = dve.scalar_tensor_tensor(
                        out=comb[:, a, c, :], in0=post_e[:, c, a, :], scalar=gain[:, k, a, c:c + 1],
                        in1=comb[:, a - 1, c, :] if a else beta_b[:, :], op0=ALU.mult, op1=ALU.add)
                last.then_inc(comb_step, 1)

            def body(t):
                if t.has(NORM):
                    k = t.slot(NORM)
                    dve.wait_ge(x_loaded[k], 16 * (t.lap(NORM) + 1))
                    for j in range(NB):
                        dve.bn_stats(stats[:, k, j, :], x_in[:, k, j, :])
                    dve.wait_ge(g_loaded[k], 32 * EB * (t.lap(NORM) + 1))
                    for c in range(2 * EB):
                        last = dve.bn_stats(stats[:, k, NB + c, :], g_in[:, k, c, 0:F])
                    last.then_inc(mean_step, 1)
                    dve.wait_ge(mean_step, 3 * t.at(NORM) + 1)
                    dve.tensor_tensor(mdiff[:, 0, :], stats[:, k, :, 1], stats[:, k, :, 4], ALU.subtract)
                    dve.tensor_tensor(mean2[:, k, :], stats[:, k, :, 1], stats[:, k, :, 4], ALU.add)
                    dve.tensor_tensor(mdiff[:, 1, :], stats[:, k, :, 2], stats[:, k, :, 5], ALU.add).then_inc(mean_step, 1)
                if t.has(TURN):
                    j, tiles = t.slot(TURN), bass.ds(t.at(TURN) * EB, EB)
                    dve.tensor_copy(gain[:, j, 0, :], g_in[:, j, EB:2 * EB, F])
                    dve.tensor_tensor(gain[:, j, 1, :], g_in[:, j, EB:2 * EB, F], amp_att[:, 0, tiles], ALU.mult)
                if t.has(NORM):
                    dve.wait_ge(mean_step, 3 * t.at(NORM) + 2)
                    dve.tensor_tensor(mdiff[:, 2, :], mdiff[:, 0, :], mdiff[:, 0, :], ALU.mult).then_inc(mean_step, 1)
                if t.has(TURN):
                    dve.tensor_tensor(gain[:, j, 2, :], g_in[:, j, EB:2 * EB, F], amp_att[:, 1, tiles], ALU.mult
                                      ).then_inc(gain_ready, 1)
                if t.has(NORM):
                    dve.wait_ge(mean_step, 3 * t.at(NORM) + 3)
                    dve.scalar_tensor_tensor(out=var[:, k, :], in0=mdiff[:, 2, :], scalar=F / 4.0, in1=mdiff[:, 1, :],
                                             op0=ALU.mult, op1=ALU.add).then_inc(var_ready, 1)
                    if not t.after(NORM):
                        scale_weights()
                if t.has(TURN):
                    dve.wait_ge(h_ready, t.at(TURN) + 1)
                    dve.tensor_tensor(xh_dst[:, j, :, :], g_in[:, j, EB:2 * EB, 0:F], hg_row[:, j, EB:2 * EB, :], ALU.add
                                      ).then_inc(xh_dst_ready, 1)
                if t.has(NORM):
                    k = t.slot(NORM)
                    dve.wait_ge(std_ready, t.at(NORM) + 1)
                    dve.reciprocal(rstd[:, k, :], std[:, k, :]).then_inc(rstd_ready, 1)
                    dve.wait_ge(rstd_ready, t.at(NORM) + 1)
                    dve.scalar_tensor_tensor(out=nmean[:, k, :], in0=mean2[:, k, :], scalar=-0.5, in1=rstd[:, k, :],
                                             op0=ALU.mult, op1=ALU.mult).then_inc(norm_ready, 1)
                    if not t.looped and t.c == NORM + 1:
                        scale_rest()
                    if not t.looped and t.c == NORM + 2:
                        list_scatters()
                if t.has(POST):
                    k = t.slot(POST)
                    dve.wait_ge(post_d_ready, t.at(POST) + 1)
                    dve.wait_ge(xh_ready, t.at(POST) + 1)
                    if t.reused(POST):
                        dve.wait_ge(y_stored[k], 16 * t.lap(POST))
                    for b in range(NB // 4):
                        rows = slice(4 * b, 4 * b + 4)
                        last = dve.scalar_tensor_tensor(out=y_out[:, k, rows, :], in0=post_d[:, rows, :], scalar=0.0,
                                                        in1=xh[:, k, rows, :], op0=ALU.max, op1=ALU.add)
                    last.then_inc(y_out_ready, 1)
                if t.has(POST):
                    dve.wait_ge(post_e_ready, t.at(POST) + 1)
                    dve.wait_ge(gain_ready, t.at(POST) + 1)
                    combine(t, 0)
                    dve.wait_ge(comb_step, 3 * t.at(POST) + 1)
                    combine(t, 1)
                if t.has(MSG):
                    k, before = t.slot(MSG), t.slot(MSG + 1)
                    end = slice(EW - 1, EW)
                    dve.wait_ge(msg_ready, t.at(MSG) + 1)
                    dve.wait_ge(edge_loaded[k], 48 * (t.lap(MSG) + 1))
                    if t.after(MSG):
                        dve.wait_ge(agg_ready, t.at(MSG))
                    dve.tensor_tensor_scan(seg_sum[:, k, :], flags[:, k, 0, :], msg_ps[:, 0:EW],
                                           seg_sum[:, before, end], ALU.mult, ALU.add).then_inc(scanned, 1)
                if t.has(POST):
                    dve.wait_ge(comb_step, 3 * t.at(POST) + 2)
                    combine(t, 2)
                if t.has(MSG):
                    dve.tensor_tensor_scan(seg_agg[:, k, 1, :], flags[:, k, 1, :], msg_ps[:, 0:EW],
                                           seg_agg[:, before, 1, end], ALU.min, ALU.max)
                    dve.tensor_tensor_scan(seg_agg[:, k, 2, :], flags[:, k, 2, :], msg_ps[:, 0:EW],
                                           seg_agg[:, before, 2, end], ALU.max, ALU.min)
                    dve.wait_ge(scanned, t.at(MSG) + 1)
                    dve.tensor_tensor(seg_agg[:, k, 0, :], seg_sum[:, k, :], rdeg[:, k, :], ALU.mult).then_inc(agg_ready, 1)
                if t.has(POST):
                    j = t.slot(POST)
                    if t.reused(POST):
                        dve.wait_ge(y_scattered[j], 32 * t.lap(POST))
                    dve.wait_ge(comb_step, 3 * t.at(POST) + 3)
                    dve.wait_ge(xh_dst_ready, t.at(POST) + 1)
                    dve.scalar_tensor_tensor(out=y_edge[:, j, :, :], in0=comb[:, 2, :, :], scalar=0.0,
                                             in1=xh_dst[:, j, :, :], op0=ALU.max, op1=ALU.add).then_inc(y_edge_ready, 1)

            run_steps(dve, NORM, POST, body)


def kernel(x, src, dst, edge_attr_16, node_vec1, L0_gnn_W_pre, L0_gnn_b_pre, L0_gnn_W_post, L0_gnn_b_post,
           L0_gnn_bn_gamma, L0_gnn_bn_beta):
    import numpy as np
    import concourse.bacc as bacc
    from concourse.bass_utils import run_bass_kernel_spmd

    x, src, dst, e, s = (np.ascontiguousarray(a) for a in (x, src, dst, edge_attr_16, node_vec1))
    dst_ext = np.full(EPAD + 2, PAD, dst.dtype)
    dst_ext[0] = dst_ext[-1] = -1
    dst_ext[1:E + 1] = dst
    src_pad = np.zeros(EPAD, src.dtype)
    src_pad[:E] = src
    e_t = np.zeros((ED, EPAD), e.dtype)
    e_t[:, :E] = e.T

    def by_slot(a):
        return np.ascontiguousarray(a.reshape(ET, P).T)

    arrays = {
        "x": x, "x_s": np.ascontiguousarray(np.concatenate([x, s], axis=1)), "snorm": s, "dst_ext": dst_ext,
        "dst_col": by_slot(dst_ext[1:EPAD + 1]), "next_col": by_slot(dst_ext[2:EPAD + 2]), "src_col": by_slot(src_pad),
        "e_t": e_t, "e_row": e, "w_pre": L0_gnn_W_pre, "b_pre": L0_gnn_b_pre, "w_post": L0_gnn_W_post, "b_post": L0_gnn_b_post,
        "gamma": L0_gnn_bn_gamma, "beta": L0_gnn_bn_beta,
    }
    arrays = {name: np.ascontiguousarray(a) for name, a in arrays.items()}
    nc = bacc.Bacc("TRN2", target_bir_lowering=False, num_devices=1)
    args = [nc.dram_tensor(name, a.shape, mybir.dt.from_np(a.dtype), kind="ExternalInput").ap()
            for name, a in arrays.items()]
    out = nc.dram_tensor("out", (N, F), F32, kind="ExternalOutput").ap()
    gnn_layer(nc, *args, out)
    return run_bass_kernel_spmd(nc, [arrays], core_ids=[0]).results[0]["out"]
```

```python
import math
from contextlib import ExitStack

import concourse.bass as bass
from concourse import mybir

F32 = mybir.dt.float32
BF16 = mybir.dt.bfloat16
I32 = mybir.dt.int32
ALU = mybir.AluOpType
ACT = mybir.ActivationFunctionType
AX_X = mybir.AxisListType.X

P = 128
N = 50000
F = 128
E = 12500
ED = 16
NB = 8
EB = 2
ROWS = NB * P
STEPS = -(-N // ROWS)
ET = EB * STEPS
EW = EB * P
EPAD = ET * P
LAST_ROW0 = N - ROWS
RING = 4
LN_EPS = 1e-5
BN_EPS = 1e-5
AVG_D_LOG = math.log(16.0)
BIG = float(2 ** 127) * (2 - 2.0 ** -7)
PAD = 65535
SKIP = 65536
GROUP_SHIFT = ROWS.bit_length() - 1
E_TERMS = (3, 2, 1)
EK = ED * sum(E_TERMS) + 3
EC = ED * EPAD // P
ECHUNK = -(-(EC + ED + 1) // 4)
S_COLS = 400
S_ROWS = N // S_COLS
assert S_ROWS * S_COLS == N and S_ROWS <= P
assert EPAD % EC == 0 and F * ED == P * ED and ECHUNK <= 512 and EK <= P
assert ET * P >= E and EPAD - E < EW and 1 << GROUP_SHIFT == ROWS

NORM, TURN, MSG, POST, CONFIRM, SCATTER = 2, 3, 4, 5, 6, 7
PREPARE = -1
AHEAD = SCATTER - CONFIRM + 1


class Step:

    def __init__(self, q, c, looped):
        self.q, self.c, self.looped = q, c, looped

    def has(self, lag):
        return self.looped or 0 <= self.c - lag < STEPS

    def at(self, lag):
        return self.q * RING + (self.c - lag)

    def slot(self, lag):
        return (self.c - lag) % RING

    def lap(self, lag):
        return self.q + (self.c - lag) // RING

    def reused(self, lag):
        return self.looped or self.c - lag >= RING

    def after(self, lag):
        return self.looped or self.c - lag >= 1


def run_steps(engine, first_lag, last_lag, body):
    begin, end = last_lag + RING, STEPS + first_lag
    turns = (end - begin) // RING
    for c in range(first_lag, begin):
        body(Step(0, c, False))
    with engine.Fori(0, turns) as q:
        for u in range(RING):
            body(Step(q, begin + u, True))
    for c in range(begin + turns * RING, STEPS + last_lag):
        body(Step(0, c, False))


def gnn_layer(nc, x, x_s, snorm, dst_ext, dst_col, next_col, src_col, e_t, e_row,
              w_pre, b_pre, w_post, b_post, gamma, beta, out):
    with ExitStack() as ctx:
        def sb(name, shape, dt=F32):
            return ctx.enter_context(nc.sbuf_tensor(name, shape, dt))

        def ps(name, shape, dt=F32):
            return ctx.enter_context(nc.psum_tensor(name, shape, dt))

        def sem(name):
            return ctx.enter_context(nc.semaphore(name))

        def sems(name):
            return [sem(f"{name}{k}") for k in range(RING)]

        flags_dram = nc.dram_tensor("flags_dram", (3, EPAD), BF16, kind="Internal").ap()
        e_dram = nc.dram_tensor("e_dram", (ED, EPAD), F32, kind="Internal").ap()
        e_terms_dram = nc.dram_tensor("e_terms_dram", (3, ED, EPAD), BF16, kind="Internal").ap()
        w_terms_dram = nc.dram_tensor("w_terms_dram", (3, ED + 1, F), BF16, kind="Internal").ap()
        late_dram = nc.dram_tensor("late_dram", (STEPS, P, EB * F), F32, kind="Internal").ap()
        sorted_dram = nc.dram_tensor("sorted_dram", (EPAD + 2, ED + 2), F32, kind="Internal").ap()
        rdeg_dram = nc.dram_tensor("rdeg_dram", (1, EPAD), F32, kind="Internal").ap()
        s_dram = nc.dram_tensor("s_dram", (3, 3, N), BF16, kind="Internal").ap()

        ident = sb("ident", [P, P])
        ones3 = sb("ones3", [3, P], BF16)
        w_msg = sb("w_msg", [P, 2, F])
        w_edge = sb("w_edge", [EK, F], BF16)
        neg_ident = sb("neg_ident", [P, P], BF16)
        e_flat = sb("e_flat", [P, EC + ED + 1])
        w_raw = sb("w_raw", [P, 10, F])
        w_h = sb("w_h", [P, F])
        w_agg = sb("w_agg", [P, 3, 3, F])
        gamma_b = sb("gamma_b", [P, F])
        scale_b = sb("scale_b", [P, F])
        beta_b = sb("beta_b", [P, F])
        b_post_1 = sb("b_post_1", [1, F])
        beta_1 = sb("beta_1", [1, F])
        bias_1 = sb("bias_1", [1, 2, F])
        rest_1 = sb("rest_1", [1, 2, 2, F])
        parts_1 = sb("parts_1", [1, 2, 3, F], BF16)
        bias3 = sb("bias3", [3, F], BF16)
        add12 = sb("add12", [12, F], BF16)
        eps_c = sb("eps_c", [P, 1])
        two_c = sb("two_c", [P, 1])
        first_table, sqrt_table = sb("first_table", [P, 1]), sb("sqrt_table", [P, 1])

        dst_i = sb("dst_i", [ET, 3, P], I32)
        flag_f = sb("flag_f", [ET, P])
        flag_n = sb("flag_n", [ET, P])
        flag_row = sb("flag_row", [ET, 3, P], BF16)
        edge_i = sb("edge_i", [ET, P], I32)
        cand = sb("cand", [ET, P])
        local = sb("local", [ET, P])
        degree = sb("degree", [ET, 2, P])
        rdeg_row = sb("rdeg_row", [ET, P])
        scaler = sb("scaler", [ET, 3, P])
        heads = sb("heads", [ET, 2])
        heads_t = sb("heads_t", [1, 2, ET])
        carry = sb("carry", [1, ET + 1])
        top_dst = sb("top_dst", [1, STEPS])
        need_i = sb("need_i", [1, 2, STEPS], I32)
        late_f = sb("late_f", [1, STEPS + 1])
        late_i = sb("late_i", [1, STEPS + 1], I32)
        cols_i = sb("cols_i", [P, 3, ET], I32)
        same_next = sb("same_next", [P, ET])
        index = sb("index", [P, STEPS, 3 * EB], I32)
        amp_att = sb("amp_att", [P, 2, ET])

        x_in = sb("x_in", [P, RING, NB, F])
        work = sb("work", [P, 4, RING, NB, F])
        h_row, xh, h_col, y_out = work[:, 0], work[:, 1], work[:, 2], work[:, 3]
        s_in = sb("s_in", [P, RING, NB])
        s_row = sb("s_row", [12, RING, ROWS], BF16)
        gather_now = sb("gather_now", [P, RING, 2 * EB], I32)
        late_now = sb("late_now", [P, EB], I32)
        late_none = sb("late_none", [1, 1 + EB, F])
        late_row = sb("late_row", [P, EB * F])
        scatter_now = sb("scatter_now", [P, RING, EB], I32)
        g_in = sb("g_in", [P, RING, 2 * EB, F + 1])
        hg_row = sb("hg_row", [P, RING, 2 * EB, F])
        hg_col = sb("hg_col", [P, RING, 2 * EB, P])
        xh_dst = sb("xh_dst", [P, RING, EB, F])
        flags = sb("flags", [P, RING, 3, EW], BF16)
        rdeg = sb("rdeg", [P, RING, EW])
        e_in = sb("e_in", [EK, RING, EW], BF16)
        gain = sb("gain", [P, RING, 3, EB])
        seg_sum = sb("seg_sum", [P, RING, EW])
        seg_agg = sb("seg_agg", [P, RING, 3, EW])
        comb = sb("comb", [P, 3, EB, F])
        y_edge = sb("y_edge", [P, RING, EB, F])
        NS = NB + 2 * EB
        stats = sb("stats", [P, RING, NS, 6])
        mean2 = sb("mean2", [P, RING, NS])
        mdiff = sb("mdiff", [P, 3, NS])
        var = sb("var", [P, RING, NS])
        std = sb("std", [P, RING, NS])
        rstd = sb("rstd", [P, RING, NS])
        nmean = sb("nmean", [P, RING, NS])

        flat = work[:, :, :, :, :].rearrange("p a r n f -> p (a r n f)")
        places = [0]

        def place(width):
            places[0] += width
            return flat[:, places[0] - width:places[0]]

        all_dst = place(EPAD)
        edge_rows = place(ET * (ED + 2)).rearrange("p (t c) -> p t c", c=ED + 2)
        less = place(EPAD // 8).bitcast(BF16)
        equal = place(P)
        earlier = place(P)
        dst_key = place(ET)
        rank_f = place(ET)
        spare = y_out.rearrange("p r n f -> p (r n f)")
        s_all = spare[0:S_ROWS, 0:S_COLS]
        s_rest = xh.rearrange("p r n f -> p (r n f)")[0:S_ROWS, 0:2 * S_COLS].rearrange("p (k c) -> p k c", k=2)
        s_terms = comb.rearrange("p a c f -> p (a c f)")[0:S_ROWS, 0:3 * S_COLS // 2].bitcast(BF16).rearrange(
            "p (k c) -> p k c", k=3)
        e_cols = EC + ED + 1
        e_terms = spare[:, NB * F:NB * F + (3 * e_cols + 1) // 2].bitcast(BF16)[:, 0:3 * e_cols].rearrange(
            "p (k c) -> p k c", k=3)
        unsorted = sb("unsorted", [ET, 2])
        unsorted_i = sb("unsorted_i", [1, 1], I32)
        order_x = sb("order_x", [ET, P])
        counts = sb("counts", [P, 5])
        rank_i = sb("rank_i", [P, ET], I32)
        rank_now = sb("rank_now", [P, 1], I32)
        edge_now = sb("edge_now", [P, ED + 2])
        ends = sb("ends", [1, ED + 2])
        dst_f = sb("dst_f", [ET, 3, P])
        cols_f = sb("cols_f", [P, 3, ET])

        turn_e = ps("turn_e", [P, 4, P])
        turn_d = ps("turn_d", [P, NB, P])
        msg_ps = ps("msg_ps", [P, 512])
        post_d = ps("post_d", [P, NB, F])
        post_e = ps("post_e", [P, EB, 4, F])

        weights_in = sem("weights_in")
        lists_in = sem("lists_in")
        set_pool = sem("set_pool")
        set_dve = sem("set_dve")
        set_act = sem("set_act")
        set_pe = sem("set_pe")
        pool_waited = sem("pool_waited")
        heads_ready, carry_ready = sem("heads_ready"), sem("carry_ready")
        gather_lists_ready, lists_ready, degree_ready = sem("gather_lists_ready"), sem("lists_ready"), sem("degree_ready")
        rows_ready, scalers_ready = sem("rows_ready"), sem("scalers_ready")
        parts_ready, w_agg_ready, set_ready = sem("parts_ready"), sem("w_agg_ready"), sem("set_ready")
        spread_out = sem("spread_out")
        e_flat_in, w_flat_in = sem("e_flat_in"), sem("w_flat_in")
        term_ready, left_ready = sem("term_ready"), sem("left_ready")
        e_terms_out, w_terms_out, w_edge_in = sem("e_terms_out"), sem("w_terms_out"), sem("w_edge_in")
        order_ready, order_known = sem("order_ready"), sem("order_known")
        s_all_in, s_split, s_spread = sem("s_all_in"), sem("s_split"), sem("s_spread")
        sort_pool, sort_dve = sem("sort_pool"), sem("sort_dve")
        sort_loaded = sem("sort_loaded")
        rank_step = sem("rank_step")
        ranked = sem("ranked")
        row_copied, row_scattered = sem("row_copied"), sem("row_scattered")
        relisted = sem("relisted")
        parts_in = sem("parts_in")
        x_loaded, s_loaded, g_loaded = sems("x_loaded"), sems("s_loaded"), sems("g_loaded")
        edge_loaded, e_loaded, s_row_loaded = sems("edge_loaded"), sems("e_loaded"), sems("s_row_loaded")
        y_stored, y_scattered = sems("y_stored"), sems("y_scattered")
        late_copied, late_loaded, late_scattered = sem("late_copied"), sem("late_loaded"), sem("late_scattered")
        index_ready, scatter_index_ready = sem("index_ready"), sem("scatter_index_ready")
        mean_step = sem("mean_step")
        var_ready = sem("var_ready")
        std_ready = sem("std_ready")
        rstd_ready = sem("rstd_ready")
        norm_ready = sem("norm_ready")
        h_ready = sem("h_ready")
        xh_ready = sem("xh_ready")
        xh_dst_ready = sem("xh_dst_ready")
        gain_ready = sem("gain_ready")
        turned_e, turned_d = sem("turned_e"), sem("turned_d")
        col_e_ready, col_d_ready = sem("col_e_ready"), sem("col_d_ready")
        msg_ready = sem("msg_ready")
        scanned = sem("scanned")
        agg_ready = sem("agg_ready")
        mm_d_ready = sem("mm_d_ready")
        scaled = sem("scaled")
        post_d_ready = sem("post_d_ready")
        post_e_ready = sem("post_e_ready")
        comb_step = sem("comb_step")
        y_edge_ready = sem("y_edge_ready")
        y_out_ready = sem("y_out_ready")
        dense_stored = sem("dense_stored")

        WEIGHTS = 16 * 7
        LISTS = 16 * 6

        def row0(step, lag):
            if not step.looped:
                return min(step.at(lag) * ROWS, LAST_ROW0)
            return step.at(lag) * ROWS

        def e_chunk(i):
            cols = slice(i * ECHUNK, min((i + 1) * ECHUNK, EC + ED + 1))
            bank = post_d[:, 4 * i:4 * i + 4, :] if i < 2 else post_e[:, i - 2, :, :]
            return bank.rearrange("p a f -> p (a f)")[:, 0:cols.stop - cols.start], cols

        block = ctx.enter_context(nc.Block())

        @block.sync
        def _(sp):
            sp.dma_start(s_all, snorm.rearrange("(p c) a -> p (c a)", c=S_COLS)).then_inc(s_all_in, 16)
            sp.dma_start(dst_i[:, 0, :], dst_ext[0:EPAD].rearrange("(t p) -> t p", p=P)).then_inc(lists_in, 16)
            sp.dma_start(dst_i[:, 1, :], dst_ext[1:EPAD + 1].rearrange("(t p) -> t p", p=P)).then_inc(lists_in, 16)
            sp.dma_start(dst_i[:, 2, :], dst_ext[2:EPAD + 2].rearrange("(t p) -> t p", p=P)).then_inc(lists_in, 16)
            def load_rows(t):
                k = t.slot(0)
                if t.reused(0):
                    sp.wait_ge(rows_ready, 1)
                    sp.wait_ge(xh_ready, t.at(0) - RING + 1)
                sp.dma_start(x_in[:, k, :, :],
                             x[bass.ds(row0(t, 0), ROWS), :].rearrange("(p r) f -> p r f", p=P)
                             ).then_inc(x_loaded[k], 16)

            def body(t):
                if not t.looped and t.c == 1:
                    sp.wait_ge(rows_ready, 1)
                if not t.looped and t.c == TURN:
                    sp.wait_ge(term_ready, 9)
                    sp.dma_start(w_terms_dram[:, 0:ED, :].rearrange("k r (q c) -> (r q) k c", c=ED),
                                 e_terms[:, :, EC:EC + ED]).then_inc(w_terms_out, 16)
                    sp.dma_start(w_terms_dram[:, ED, :].rearrange("k (p a) -> p k a", a=1),
                                 e_terms[:, :, EC + ED:EC + ED + 1],
                                 allow_slow_non_contiguous=True).then_inc(w_terms_out, 16)
                    for k in range(3):
                        sp.dma_start(e_terms_dram[k].rearrange("r (q c) -> (r q) c", c=EC), e_terms[:, k, 0:EC]
                                      ).then_inc(e_terms_out, 16)
                if t.has(0) and (t.looped or t.c != TURN):
                    load_rows(t)
                if t.has(NORM):
                    k = t.slot(NORM)
                    if t.reused(NORM):
                        sp.wait_ge(rows_ready, 1)
                        sp.wait_ge(post_d_ready, t.at(NORM) - RING + 1)
                        sp.wait_ge(agg_ready, t.at(NORM) - RING + 1)
                    elif t.c == NORM:
                        sp.wait_ge(spread_out, 32)
                    sp.dma_start(s_in[:, k, :],
                                 snorm[bass.ds(row0(t, NORM), ROWS), :].rearrange("(p r) a -> p (r a)", p=P)
                                 ).then_inc(s_loaded[k], 16)
                    e0 = t.at(NORM) * EW
                    sp.dma_start(flags[:, k, :, :],
                                 flags_dram[:, bass.ds(e0, EW)].partition_broadcast(P)).then_inc(edge_loaded[k], 16)
                    sp.dma_start(rdeg[:, k, :],
                                 rdeg_dram[:, bass.ds(e0, EW)].partition_broadcast(P)).then_inc(edge_loaded[k], 16)
                if not t.looped and t.c == TURN:
                    sp.wait_ge(w_terms_out, 32)
                    row = 0
                    for terms in E_TERMS:
                        sp.dma_start(w_edge[row:row + terms * ED, :], w_terms_dram[0:terms, 0:ED, :]).then_inc(w_edge_in, 16)
                        row += terms * ED
                    sp.dma_start(w_edge[row:row + 3, :], w_terms_dram[:, ED, :]).then_inc(w_edge_in, 16)
                    sp.wait_ge(e_terms_out, 48)
                if t.has(TURN):
                    k = t.slot(TURN)
                    if t.reused(TURN):
                        sp.wait_ge(rows_ready, 1)
                        sp.wait_ge(agg_ready, t.at(TURN) - RING + 1)
                        sp.wait_ge(post_d_ready, t.at(TURN) - RING + 1)
                    row = 0
                    for term, copies in enumerate(E_TERMS):
                        rows = e_terms_dram[term:term + 1, :, bass.ds(t.at(TURN) * EW, EW)]
                        sp.dma_start(e_in[row:row + copies * ED, k, :], rows.broadcast_to((copies, ED, EW))
                                     ).then_inc(e_loaded[k], 16)
                        row += copies * ED
                if not t.looped and t.c == TURN:
                    sp.wait_ge(parts_ready, 1)
                    sp.dma_start(bias3[:, :], parts_1[0:1, 0, :, :]).then_inc(parts_in, 16)
                    for r in range(3):
                        sp.dma_start(add12[3 * r:3 * r + 3, :], parts_1[0:1, 0, :, :]).then_inc(parts_in, 16)
                    sp.dma_start(add12[9:12, :], parts_1[0:1, 1, :, :]).then_inc(parts_in, 16)
                    load_rows(t)
                    sp.wait_ge(s_split, 5)
                    for r in range(3):
                        sp.dma_start(s_dram[r].rearrange("k (p c) -> p k c", c=S_COLS),
                                     s_terms[:, r:r + 1, :].broadcast_to((S_ROWS, 3, S_COLS))
                                     ).then_inc(s_spread, 16)
                    sp.wait_ge(s_spread, 48)
                if t.has(TURN):
                    sp.dma_start(s_row[0:9, k, :],
                                 s_dram.rearrange("r k n -> (r k) n")[:, bass.ds(row0(t, TURN), ROWS)]
                                 ).then_inc(s_row_loaded[k], 16)
                if t.has(CONFIRM):
                    sp.wait_ge(rows_ready, 1)
                    sp.wait_ge(y_stored[t.slot(CONFIRM)], 16 * (t.lap(CONFIRM) + 1))
                    sp.sem_inc(dense_stored, 1)
                if t.has(POST):
                    k = t.slot(POST)
                    sp.wait_ge(y_out_ready, t.at(POST) + 1)
                    if not t.looped and t.c - POST == STEPS - 1:
                        sp.wait_ge(y_stored[(k - 1) % RING], 16 * (t.lap(POST + 1) + 1))
                    sp.dma_start(out[bass.ds(row0(t, POST), ROWS), :].rearrange("(p r) f -> p r f", p=P),
                                 y_out[:, k, :, :]).then_inc(y_stored[k], 16)

            run_steps(sp, 0, CONFIRM, body)

        def scatter_late(pool):
            with pool.Fori(0, STEPS) as j:
                with pool.If(pool.value_load(late_i[0:1, bass.ds(j, 1)], min_val=0, max_val=1) > 0):
                    pool.tensor_copy(late_now[:, :], index[:, bass.ds(j, 1), 2 * EB:3 * EB].rearrange("p a c -> p (a c)")
                                     ).then_inc(late_copied, 1)
                    pool.dma_start(late_row[:, :], late_dram[bass.ds(j, 1), :, :].rearrange("a p f -> (a p) f")
                                   ).then_inc(late_loaded, 16)
                    pool.wait_ge(late_copied, j + 1)
                    pool.wait_ge(late_loaded, j * 16 + 16)
                    pool.sem_inc(pool_waited, 1)
                    for c in range(EB):
                        pool.indirect_dma_start(out, bass.IndirectOffsetOnAxis(late_now[:, c:c + 1], 0),
                                                late_row[:, c * F:(c + 1) * F], None, bounds_check=N - 1, oob_is_err=False,
                                                ).then_inc(late_scattered, 16)
                with pool.Else():
                    pool.sem_inc(late_copied, 1)
                    pool.dma_start(late_none[:, 0, :], beta.rearrange("(a f) -> a f", a=1)).then_inc(late_loaded, 16)
                    for c in range(EB):
                        pool.dma_start(late_none[:, 1 + c, :], beta.rearrange("(a f) -> a f", a=1)
                                       ).then_inc(late_scattered, 16)
                    pool.wait_ge(late_loaded, j * 16 + 16)
                pool.wait_ge(late_scattered, j * (16 * EB) + 16 * EB)

        SORT_LOADS = 16 * 3
        RELISTS = 16 * (6 + ED)

        def put_in_order(pool):
            pool.wait_ge(s_split, 5)
            pool.memset(edge_rows[:, :, :], 0.0).then_inc(sort_pool, 1)
            pool.memset(ends[:, :], -1.0).then_inc(sort_pool, 1)
            pool.memset(earlier[:, :], 1.0).then_inc(sort_pool, 1)
            pool.wait_ge(sort_pool, 3)
            pool.affine_select(out=earlier[:, :], in_=earlier[:, :], compare_op=ALU.is_gt, fill=0.0,
                               base=0, pattern=[[-1, P]], channel_multiplier=1).then_inc(sort_pool, 1)
            pool.dma_start(all_dst.bitcast(I32), dst_ext[1:EPAD + 1].rearrange("(a e) -> a e", a=1).partition_broadcast(P)
                           ).then_inc(sort_loaded, 16)
            full = E // P
            pool.dma_start(edge_rows[:, 0:full, 0:ED], e_row[0:full * P, :].rearrange("(t p) c -> p t c", p=P)
                           ).then_inc(sort_loaded, 16)
            pool.dma_start(edge_rows[0:E - full * P, full, 0:ED], e_row[full * P:E, :]).then_inc(sort_loaded, 16)
            pool.dma_start(sorted_dram[0:1, :], ends[:, :]).then_inc(row_scattered, 16)
            pool.dma_start(sorted_dram[EPAD + 1:EPAD + 2, :], ends[:, :]).then_inc(row_scattered, 16)
            pool.wait_ge(ranked, 1)
            with pool.Fori(0, ET) as t:
                pool.tensor_copy(rank_now[:, :], rank_i[:, bass.ds(t, 1)]).then_inc(row_copied, 1)
                pool.tensor_copy(edge_now[:, :], edge_rows[:, bass.ds(t, 1), :].rearrange("p a c -> p (a c)")
                                 ).then_inc(row_copied, 1)
                pool.wait_ge(row_copied, t * 2 + 2)
                pool.sem_inc(pool_waited, 1)
                pool.indirect_dma_start(sorted_dram, bass.IndirectOffsetOnAxis(rank_now[:, 0:1], 0),
                                        edge_now[:, :], None).then_inc(row_scattered, 16)
                pool.wait_ge(row_scattered, t * 16 + 48)
            for shift in range(3):
                rows = sorted_dram[shift:shift + EPAD, ED:ED + 1]
                pool.dma_start(dst_f[:, shift, :], rows.rearrange("(t p) c -> t (p c)", p=P),
                               allow_slow_non_contiguous=True).then_inc(relisted, 16)
            for col, (shift, what) in enumerate([(1, ED + 1), (1, ED), (2, ED)]):
                rows = sorted_dram[shift:shift + EPAD, what:what + 1]
                pool.dma_start(cols_f[:, col, :], rows.rearrange("(t p) c -> p (t c)", p=P),
                               allow_slow_non_contiguous=True).then_inc(relisted, 16)
            for c in range(ED):
                pool.dma_start(e_dram[c:c + 1, :].rearrange("a (t p) -> (a t) p", p=P),
                               sorted_dram[1:EPAD + 1, c:c + 1].rearrange("(t p) c -> t (p c)", p=P),
                               allow_slow_non_contiguous=True).then_inc(relisted, 16)
            pool.wait_ge(relisted, RELISTS)
            pool.dma_start(e_flat[:, 0:EC], e_dram.rearrange("r (q c) -> (r q) c", c=EC)).then_inc(e_flat_in, 16)

        @block.gpsimd
        def _(pool):
            pool.memset(ident[:, :], 0.0).then_inc(set_pool, 1)
            pool.wait_ge(set_pool, 1)
            pool.affine_select(out=ident[:, :], in_=ident[:, :], compare_op=ALU.not_equal, fill=1.0,
                               base=0, pattern=[[-1, P]], channel_multiplier=1).then_inc(set_pool, 1)
            pool.wait_ge(set_pool, 2)
            pool.tensor_scalar(neg_ident[:, :], ident[:, :], -1.0, None, ALU.mult).then_inc(set_pool, 1)
            pool.memset(e_in[:, :, :], 1.0).then_inc(set_pool, 1)
            pool.memset(s_row[:, :, :], 1.0).then_inc(set_pool, 1)
            pool.iota(edge_i[:, :], pattern=[[1, P]], base=0, channel_multiplier=P).then_inc(set_pool, 1)
            pool.wait_ge(order_known, 1)
            with pool.If(pool.value_load(unsorted_i[0:1, 0:1], min_val=0, max_val=1) > 0):
                put_in_order(pool)
            with pool.Else():
                pool.dma_start(e_flat[:, 0:EC], e_t.rearrange("r (q c) -> (r q) c", c=EC)).then_inc(e_flat_in, 16)
                pool.sem_inc(sort_pool, 1)
            pool.wait_ge(gather_lists_ready, 1)

            def body(t):
                if t.has(0):
                    k = t.slot(0)
                    if t.reused(0):
                        pool.wait_ge(xh_dst_ready, t.at(0) - RING + 1)
                        pool.wait_ge(xh_ready, t.at(0) - RING + 1)
                    pool.wait_ge(index_ready, t.at(0) + 1)
                    pool.sem_inc(pool_waited, 1)
                    for c in range(2 * EB):
                        pool.indirect_dma_start(g_in[:, k, c, :], None, x_s,
                                                bass.IndirectOffsetOnAxis(gather_now[:, k, c:c + 1], 0),
                                                ).then_inc(g_loaded[k], 16)
                if t.has(PREPARE):
                    k = t.slot(PREPARE)
                    if t.reused(PREPARE):
                        pool.wait_ge(norm_ready, t.at(PREPARE) - RING + 1)
                    pool.tensor_copy(gather_now[:, k, :],
                                     index[:, bass.ds(t.at(PREPARE), 1), 0:2 * EB].rearrange("p a c -> p (a c)")
                                     ).then_inc(index_ready, 1)
                if t.has(SCATTER):
                    k = t.slot(SCATTER)
                    if not t.after(SCATTER):
                        pool.wait_ge(lists_ready, 1)
                    if t.reused(SCATTER):
                        pool.wait_ge(y_scattered[k], 32 * t.lap(SCATTER))
                    pool.tensor_copy(scatter_now[:, k, :],
                                     index[:, bass.ds(t.at(SCATTER), 1), 2 * EB:3 * EB].rearrange("p a c -> p (a c)")
                                     ).then_inc(scatter_index_ready, 1)
                    late = pool.value_load(late_i[0:1, bass.ds(t.at(SCATTER), 1)], min_val=0, max_val=1)
                if t.has(TURN):
                    k = t.slot(TURN)
                    pool.wait_ge(h_ready, t.at(TURN) + 1)
                    if t.reused(TURN):
                        pool.wait_ge(y_out_ready, t.at(TURN) - RING + 1)
                    pool.tensor_tensor(xh[:, k, :, :], x_in[:, k, :, :], h_row[:, k, :, :], ALU.add).then_inc(xh_ready, 1)
                if t.has(SCATTER):
                    k = t.slot(SCATTER)
                    pool.wait_ge(scatter_index_ready, t.at(SCATTER) + 1)
                    pool.wait_ge(y_edge_ready, t.at(SCATTER) + 1)
                    pool.wait_ge(dense_stored, t.at(SCATTER) + AHEAD if t.looped else min(t.at(SCATTER) + AHEAD, STEPS))
                    pool.sem_inc(pool_waited, 1)
                    with pool.If(late > 0):
                        for c in range(EB):
                            pool.dma_start(late_dram[bass.ds(t.at(SCATTER), 1), :, c * F:(c + 1) * F].rearrange("a p f -> (a p) f"),
                                           y_edge[:, k, c, :]).then_inc(y_scattered[k], 16)
                    with pool.Else():
                        for c in range(EB):
                            pool.indirect_dma_start(out, bass.IndirectOffsetOnAxis(scatter_now[:, k, c:c + 1], 0),
                                                    y_edge[:, k, c, :], None, bounds_check=N - 1, oob_is_err=False,
                                                    ).then_inc(y_scattered[k], 16)

            run_steps(pool, PREPARE, SCATTER, body)
            late = pool.value_load(late_i[0:1, STEPS:STEPS + 1], min_val=0, max_val=1)
            for k in range(RING):
                pool.wait_ge(y_scattered[k], 32 * len(range(k, STEPS, RING)))
            pool.wait_ge(dense_stored, STEPS)
            with pool.If(late > 0):
                scatter_late(pool)
            with pool.Else():
                pool.sem_inc(pool_waited, 1)

        @block.tensor
        def _(pe):
            pe.wait_ge(set_pool, 2)
            pe.wait_ge(order_ready, 1)
            pe.transpose(turn_e[0:1, 0, 0:ET], unsorted[:, 0:1], ident[0:ET, 0:ET]).then_inc(set_pe, 1)
            pe.wait_ge(heads_ready, 1)
            pe.transpose(msg_ps[0:1, 0:ET], heads[:, 0:1], ident[0:ET, 0:ET])
            pe.transpose(msg_ps[0:1, P:P + ET], heads[:, 1:2], ident[0:ET, 0:ET]).then_inc(set_pe, 1)
            pe.wait_ge(carry_ready, 1)
            pe.transpose(msg_ps[0:ET, 2 * P:2 * P + 1], carry[0:1, 0:ET], ident[0:1, 0:1]).then_inc(set_pe, 1)
            pe.wait_ge(set_pool, 3)
            pe.wait_ge(e_flat_in, 16)
            pe.wait_ge(w_flat_in, 32)
            pe.wait_ge(term_ready, 1)
            for i in range(4):
                bank, cols = e_chunk(i)
                pe.matmul(bank, ident[:, :], e_flat[:, cols], start=True, stop=False, skip_group_check=True)
                pe.matmul(bank, neg_ident[:, :], e_terms[:, 0, cols], start=False, stop=True, skip_group_check=True
                          ).then_inc(left_ready, 1)
            for i in range(4):
                bank, cols = e_chunk(i)
                pe.wait_ge(term_ready, 2 + i)
                pe.matmul(bank, neg_ident[:, :], e_terms[:, 1, cols], start=False, stop=True, skip_group_check=True
                          ).then_inc(left_ready, 1)
            pe.wait_ge(scalers_ready, 1)
            pe.transpose(msg_ps[:, 0:ET], scaler[:, 1, :], ident[0:ET, 0:ET])
            pe.transpose(msg_ps[:, P:P + ET], scaler[:, 2, :], ident[0:ET, 0:ET]).then_inc(set_pe, 1)

            def body(t):
                if not t.after(POST) and t.has(POST):
                    pe.wait_ge(parts_in, 16 * 5)
                    pe.wait_ge(w_agg_ready, 1)
                if t.has(POST):
                    k = t.slot(POST)
                    pe.wait_ge(agg_ready, t.at(POST) + 1)
                    if t.after(POST):
                        pe.wait_ge(comb_step, 3 * t.at(POST))
                    for c in range(EB):
                        pe.matmul(post_e[:, c, 0, :], ones3[:, :], bias3[:, :], start=True, stop=False,
                                  skip_group_check=True)
                        pe.matmul(post_e[:, c, 0, :], hg_col[:, k, EB + c, :], w_h[:, :], start=False, stop=False,
                                  skip_group_check=True)
                        for a in range(3):
                            last = pe.matmul(post_e[:, c, 0:3, :], seg_agg[:, k, a, c * P:(c + 1) * P], w_agg[:, a, :, :],
                                             start=False, stop=(a == 2), skip_group_check=True)
                        if c == 0:
                            pe.wait_ge(s_row_loaded[k], 16 * (t.lap(POST) + 1))
                            pe.wait_ge(scaled, t.at(POST) + 1)
                            for j in range(NB):
                                rows = s_row[:, k, :].rearrange("a (p r) -> a r p", r=NB)[:, j, :]
                                added = pe.matmul(post_d[:, j, :], rows, add12[:, :],
                                                  start=False, stop=(j % 4 == 3), skip_group_check=True)
                            added.then_inc(post_d_ready, 1)
                    last.then_inc(post_e_ready, 1)
                if not t.after(MSG) and t.has(MSG):
                    pe.wait_ge(set_ready, 1)
                    pe.wait_ge(weights_in, WEIGHTS)
                    pe.wait_ge(w_edge_in, 16 * 4)
                    pe.wait_ge(term_ready, 9)
                if t.has(MSG):
                    k = t.slot(MSG)
                    pe.wait_ge(col_e_ready, t.at(MSG) + 1)
                    pe.wait_ge(e_loaded[k], 48 * (t.lap(MSG) + 1))
                    if t.after(MSG):
                        pe.wait_ge(agg_ready, t.at(MSG))
                    pe.matmul(msg_ps[:, 0:EW], w_msg[:, 0, :], hg_col[:, k, 0:EB, :], start=True, stop=False)
                    pe.matmul(msg_ps[:, 0:EW], w_msg[:, 1, :], hg_col[:, k, EB:2 * EB, :], start=False, stop=False)
                    pe.matmul(msg_ps[:, 0:EW], w_edge[:, :], e_in[:, k, :], start=False, stop=True
                              ).then_inc(msg_ready, 1)
                    pe.wait_ge(col_d_ready, t.at(MSG) + 1)
                    if t.after(MSG):
                        pe.wait_ge(y_out_ready, t.at(MSG))
                    for j in range(NB):
                        last = pe.matmul(post_d[:, j, :], h_col[:, k, j, :], w_h[:, :],
                                         start=(j % 4 == 0), stop=False, skip_group_check=True)
                    last.then_inc(mm_d_ready, 1)
                if t.has(TURN):
                    k = t.slot(TURN)
                    pe.wait_ge(h_ready, t.at(TURN) + 1)
                    if t.after(TURN):
                        pe.wait_ge(col_e_ready, t.at(TURN))
                        pe.wait_ge(col_d_ready, t.at(TURN))
                    for c in range(2 * EB):
                        last = pe.transpose(turn_e[:, c, :], hg_row[:, k, c, :], ident[:, :])
                    last.then_inc(turned_e, 1)
                    for j in range(NB):
                        last = pe.transpose(turn_d[:, j, :], h_row[:, k, j, :], ident[:, :])
                    last.then_inc(turned_d, 1)

            run_steps(pe, TURN, POST, body)

        @block.scalar
        def _(act):
            act.dma_start(cols_i[:, 0, :], src_col).then_inc(lists_in, 16)
            act.dma_start(cols_i[:, 1, :], dst_col).then_inc(lists_in, 16)
            act.dma_start(cols_i[:, 2, :], next_col).then_inc(lists_in, 16)
            act.dma_start(e_flat[:, EC:EC + ED], w_pre[2 * P:2 * P + ED, :].rearrange("r (q c) -> (r q) c", c=ED)
                          ).then_inc(w_flat_in, 16)
            act.dma_start(e_flat[:, EC + ED:EC + ED + 1], b_pre.rearrange("(p a) -> p a", a=1)).then_inc(w_flat_in, 16)
            act.dma_start(gamma_b[:, :], gamma.rearrange("(a f) -> a f", a=1).partition_broadcast(P)).then_inc(weights_in, 16)
            act.dma_start(w_raw[:, :, :], w_post.rearrange("(b k) f -> k b f", k=P)).then_inc(weights_in, 16)
            act.dma_start(beta_b[:, :], beta.rearrange("(a f) -> a f", a=1).partition_broadcast(P)).then_inc(weights_in, 16)
            act.dma_start(b_post_1[:, :], b_post.rearrange("(a f) -> a f", a=1)).then_inc(weights_in, 16)
            act.dma_start(beta_1[:, :], beta.rearrange("(a f) -> a f", a=1)).then_inc(weights_in, 16)
            act.dma_start(w_msg[:, 0, :], w_pre[0:P, :]).then_inc(weights_in, 16)
            act.dma_start(w_msg[:, 1, :], w_pre[P:2 * P, :]).then_inc(weights_in, 16)

            act.wait_ge(set_dve, 3)
            nc.scalar.activation(first_table[:, :], two_c[:, :], ACT.Ln).then_inc(set_act, 1)
            act.wait_ge(w_flat_in, 32)
            act.wait_ge(e_flat_in, 16)
            nc.scalar.activation(e_terms[:, 0, :], e_flat[:, :], ACT.Copy).then_inc(term_ready, 1)
            act.wait_ge(degree_ready, 1)
            nc.scalar.activation(scaler[:, 0, :], degree[:, 0, :], ACT.Ln, bias=two_c[0:ET, 0:1]).then_inc(set_act, 1)
            nc.scalar.activation(sqrt_table[:, :], two_c[:, :], ACT.Sqrt).then_inc(set_act, 1)
            act.wait_ge(rows_ready, 1)
            act.dma_start(flags_dram.rearrange("c (t p) -> t c p", p=P), flag_row[:, :, :]).then_inc(spread_out, 16)
            act.dma_start(rdeg_dram.rearrange("a (t p) -> (a t) p", p=P), rdeg_row[:, :]).then_inc(spread_out, 16)

            def last_terms():
                for i in range(4):
                    bank, cols = e_chunk(i)
                    act.wait_ge(left_ready, 1 + i)
                    nc.scalar.activation(e_terms[:, 1, cols], bank, ACT.Copy).then_inc(term_ready, 1)
                for i in range(4):
                    bank, cols = e_chunk(i)
                    act.wait_ge(left_ready, 5 + i)
                    nc.scalar.activation(e_terms[:, 2, cols], bank, ACT.Copy).then_inc(term_ready, 1)
            def body(t):
                if t.has(POST):
                    k = t.slot(POST)
                    act.wait_ge(s_loaded[k], 16 * (t.lap(POST) + 1))
                    act.wait_ge(mm_d_ready, t.at(POST) + 1)
                    for j in range(NB):
                        last = nc.scalar.activation(post_d[:, j, :], post_d[:, j, :], ACT.Copy, scale=s_in[:, k, j:j + 1])
                    last.then_inc(scaled, 1)
                if t.has(MSG):
                    k = t.slot(MSG)
                    act.wait_ge(turned_e, t.at(MSG) + 1)
                    nc.scalar.activation(hg_col[:, k, :, :], turn_e[:, :, :], ACT.Copy).then_inc(col_e_ready, 1)
                if t.has(NORM):
                    k = t.slot(NORM)
                    act.wait_ge(var_ready, t.at(NORM) + 1)
                    nc.scalar.activation(std[:, k, :], var[:, k, :], ACT.Sqrt, bias=eps_c[:, 0:1], scale=1.0 / F
                                         ).then_inc(std_ready, 1)
                    if not t.after(NORM):
                        last_terms()
                if t.has(MSG):
                    k = t.slot(MSG)
                    act.wait_ge(turned_d, t.at(MSG) + 1)
                    for b in range(NB // 4):
                        last = nc.scalar.activation(h_col[:, k, 4 * b:4 * b + 4, :], turn_d[:, 4 * b:4 * b + 4, :], ACT.Copy)
                    last.then_inc(col_d_ready, 1)
                if t.has(NORM):
                    k = t.slot(NORM)
                    act.wait_ge(norm_ready, t.at(NORM) + 1)
                    if t.reused(NORM):
                        act.wait_ge(xh_dst_ready, t.at(NORM) - RING + 1)
                        act.wait_ge(xh_ready, t.at(NORM) - RING + 1)
                        act.wait_ge(turned_d, t.at(NORM) - RING + 1)
                    for c in range(2 * EB):
                        nc.scalar.activation(hg_row[:, k, c, :], g_in[:, k, c, 0:F], ACT.Relu,
                                             bias=nmean[:, k, NB + c:NB + c + 1], scale=rstd[:, k, NB + c:NB + c + 1])
                    for j in range(NB):
                        last = nc.scalar.activation(h_row[:, k, j, :], x_in[:, k, j, :], ACT.Relu,
                                                    bias=nmean[:, k, j:j + 1], scale=rstd[:, k, j:j + 1])
                    last.then_inc(h_ready, 1)

            run_steps(act, NORM, POST, body)

        def rank_edges(dve):
            dve.wait_ge(sort_loaded, SORT_LOADS)
            dve.wait_ge(sort_pool, 4)
            dve.tensor_copy(all_dst, all_dst.bitcast(I32)).then_inc(sort_dve, 1)
            dve.tensor_copy(dst_key, cols_i[:, 1, :]).then_inc(sort_dve, 1)
            dve.tensor_copy(edge_rows[:, :, ED], cols_i[:, 1, :]).then_inc(sort_dve, 1)
            dve.tensor_copy(edge_rows[:, :, ED + 1], cols_i[:, 0, :]).then_inc(sort_dve, 1)
            dve.wait_ge(sort_dve, 4)
            quarter = EPAD // 4
            with dve.Fori(0, ET) as t:
                key = dst_key[:, bass.ds(t, 1)]
                tile = all_dst[:, bass.ds(t * P, P)]
                for c in range(4):
                    dve.tensor_scalar(less, all_dst[:, c * quarter:(c + 1) * quarter], key, None, ALU.is_lt, ALU.add,
                                      accum_out=counts[:, c:c + 1]).then_inc(rank_step, 1)
                    dve.wait_ge(rank_step, t * 7 + (c + 1))
                dve.scalar_tensor_tensor(out=equal, in0=tile, scalar=key, in1=earlier, op0=ALU.is_equal, op1=ALU.mult,
                                         accum_out=counts[:, 4:5]).then_inc(rank_step, 1)
                dve.wait_ge(rank_step, t * 7 + 5)
                dve.tensor_reduce(rank_f[:, bass.ds(t, 1)], counts[:, :], AX_X, ALU.add).then_inc(rank_step, 1)
                dve.tensor_scalar(tile, tile, -0.5, None, ALU.add).then_inc(rank_step, 1)
                dve.wait_ge(rank_step, t * 7 + 7)
            dve.tensor_scalar(rank_i[:, :], rank_f, 1.0, None, ALU.add).then_inc(ranked, 1)
            dve.wait_ge(relisted, RELISTS)
            dve.tensor_copy(dst_i[:, :, :], dst_f[:, :, :]).then_inc(sort_dve, 1)
            dve.tensor_copy(cols_i[:, :, :], cols_f[:, :, :]).then_inc(sort_dve, 1)
            dve.wait_ge(sort_dve, 6)

        @block.vector
        def _(dve):
            done = [0]

            def then(ins):
                done[0] += 1
                return ins.then_inc(set_dve, 1)

            def chain(ins):
                then(ins)
                dve.wait_ge(set_dve, done[0])

            def mark(reached):
                dve.wait_ge(set_dve, done[0])
                dve.sem_inc(reached, 1)

            then(dve.memset(ones3[:, :], 1.0))
            then(dve.memset(eps_c[:, :], LN_EPS))
            then(dve.memset(two_c[:, :], 2.0))
            then(dve.memset(seg_sum[:, RING - 1, EW - 1:EW], 0.0))
            then(dve.memset(seg_agg[:, RING - 1, :, EW - 1:EW], 0.0))
            chain(dve.memset(carry[:, :], 0.0))
            dve.wait_ge(s_all_in, 16)
            left = s_all
            for k in range(3):
                dve.tensor_copy(s_terms[:, k, :], left).then_inc(s_split, 1)
                if k < 2:
                    dve.wait_ge(s_split, 2 * k + 1)
                    dve.tensor_tensor(s_rest[:, k, :], left, s_terms[:, k, :], ALU.subtract).then_inc(s_split, 1)
                    dve.wait_ge(s_split, 2 * k + 2)
                    left = s_rest[:, k, :]
            dve.wait_ge(lists_in, LISTS)
            chain(dve.tensor_tensor(order_x[:, :], dst_i[:, 0, :], dst_i[:, 1, :], ALU.is_gt))
            chain(dve.tensor_reduce(unsorted[:, 0:1], order_x[:, :], AX_X, ALU.max))
            mark(order_ready)
            dve.wait_ge(set_pe, 1)
            chain(dve.tensor_reduce(unsorted_i[:, :], turn_e[0:1, 0, 0:ET], AX_X, ALU.max))
            mark(order_known)
            with dve.If(dve.value_load(unsorted_i[0:1, 0:1], min_val=0, max_val=1) > 0):
                rank_edges(dve)
            with dve.Else():
                dve.sem_inc(sort_dve, 1)
            def pairs(a):
                return a.rearrange("p (j c) -> p j c", c=EB)
            then(dve.tensor_copy(index[:, :, 0:EB], pairs(cols_i[:, 0, :])))
            then(dve.tensor_scalar(index[:, :, EB:2 * EB], pairs(cols_i[:, 1, :]), float(N - 1), None, ALU.min))
            mark(gather_lists_ready)
            chain(dve.tensor_tensor(flag_f[:, :], dst_i[:, 0, :], dst_i[:, 1, :], ALU.is_equal))
            then(dve.tensor_copy(flag_row[:, 0, :], flag_f[:, :]))
            chain(dve.tensor_scalar(flag_n[:, :], flag_f[:, :], -1.0, BIG, ALU.add, ALU.mult))
            chain(dve.scalar_tensor_tensor(out=local[:, :], in0=flag_f[:, :], scalar=BIG, in1=flag_n[:, :],
                                           op0=ALU.mult, op1=ALU.add))
            then(dve.tensor_copy(flag_row[:, 1, :], local[:, :]))
            chain(dve.tensor_scalar(flag_row[:, 2, :], local[:, :], -1.0, None, ALU.mult))
            dve.wait_ge(set_pool, 6)
            chain(dve.scalar_tensor_tensor(out=flag_n[:, :], in0=flag_f[:, :], scalar=1.0, in1=edge_i[:, :],
                                           op0=ALU.is_lt, op1=ALU.mult))
            chain(dve.tensor_tensor_scan(local[:, :], flag_n[:, :], flag_n[:, :], 0.0, ALU.max, ALU.max))
            then(dve.tensor_copy(heads[:, 0:1], local[:, P - 1:P]))
            chain(dve.tensor_reduce(heads[:, 1:2], dst_i[:, 1, :], AX_X, ALU.max))
            mark(heads_ready)
            dve.wait_ge(set_pe, 2)
            chain(dve.tensor_copy(heads_t[:, :, :], msg_ps[0:1, 0:2 * P].rearrange("a (b t) -> a b t", b=2)[:, :, 0:ET]))
            chain(dve.tensor_tensor_scan(carry[0:1, 1:ET + 1], heads_t[:, 0, :], heads_t[:, 0, :], 0.0, ALU.max, ALU.max))
            mark(carry_ready)
            dve.wait_ge(set_pe, 3)
            chain(dve.tensor_scalar(cand[:, :], local[:, :], msg_ps[0:ET, 2 * P:2 * P + 1], None, ALU.max))
            chain(dve.tensor_tensor(degree[:, 0, :], edge_i[:, :], cand[:, :], ALU.subtract))
            mark(degree_ready)
            chain(dve.tensor_scalar(degree[:, 1, :], degree[:, 0, :], 1.0, None, ALU.add))
            chain(dve.reciprocal(rdeg_row[:, :], degree[:, 1, :]))
            mark(rows_ready)
            def scale_weights():
                dve.wait_ge(set_act, 2)
                then(dve.tensor_scalar(scaler[:, 1, :], scaler[:, 0, :], 1.0 / AVG_D_LOG, None, ALU.mult))
                chain(dve.reciprocal(cand[:, :], scaler[:, 0, :]))
                chain(dve.tensor_scalar(scaler[:, 2, :], cand[:, :], AVG_D_LOG, None, ALU.mult))
                mark(scalers_ready)
                dve.wait_ge(weights_in, WEIGHTS)
                chain(dve.tensor_scalar(scale_b[:, :], gamma_b[:, :], 1.0 / math.sqrt(1.0 + BN_EPS), None, ALU.mult))
                then(dve.tensor_tensor(w_h[:, :], w_raw[:, 0, :], scale_b[:, :], ALU.mult))

            def scale_rest():
                w_post_agg = w_raw[:, 1:10, :].rearrange("p (c a) f -> p c a f", a=3)
                then(dve.tensor_tensor(w_agg[:, :, :, :].rearrange("p a c f -> p c a f"), w_post_agg,
                                       scale_b[:, :].rearrange("p (a c f) -> p a c f", a=1, c=1).broadcast_to((P, 3, 3, F)),
                                       ALU.mult))
                mark(w_agg_ready)

            def split_bias():
                then(dve.tensor_tensor(bias_1[:, 0, :], b_post_1[:, :], scale_b[0:1, :], ALU.mult))
                chain(dve.tensor_copy(bias_1[:, 1, :], beta_1[:, :]))
                src = bias_1[:, :, :]
                for k in range(3):
                    chain(dve.tensor_copy(parts_1[:, :, k, :], src))
                    if k < 2:
                        chain(dve.tensor_tensor(rest_1[:, k, :, :], src, parts_1[:, :, k, :], ALU.subtract))
                        src = rest_1[:, k, :, :]
                mark(parts_ready)

            def list_scatters():
                chain(dve.tensor_tensor(same_next[:, :], cols_i[:, 1, :], cols_i[:, 2, :], ALU.is_equal))
                then(dve.scalar_tensor_tensor(out=index[:, :, 2 * EB:3 * EB], in0=pairs(same_next[:, :]), scalar=float(SKIP),
                                              in1=pairs(cols_i[:, 1, :]), op0=ALU.mult, op1=ALU.add))
                chain(dve.tensor_reduce(top_dst[:, :], heads_t[:, 1, :].rearrange("a (j c) -> a j c", c=EB), AX_X, ALU.max))
                chain(dve.tensor_scalar(need_i[:, 0, :], top_dst[:, :], float(N - 1), float(STEPS * ROWS - N + ROWS),
                                        ALU.min, ALU.add))
                chain(dve.tensor_scalar(need_i[:, 1, :], need_i[:, 0, :], GROUP_SHIFT, None, ALU.logical_shift_right))
                chain(dve.scalar_tensor_tensor(out=late_f[:, 0:STEPS], in0=need_i[:, 1, :], scalar=-float(AHEAD),
                                               in1=edge_i[0:1, 0:STEPS], op0=ALU.add, op1=ALU.is_gt))
                chain(dve.tensor_reduce(late_f[:, STEPS:STEPS + 1], late_f[:, 0:STEPS], AX_X, ALU.max))
                then(dve.tensor_copy(late_i[:, :], late_f[:, :]))
                mark(lists_ready)

            def finish_rows(t, b):
                k, rows = t.slot(POST), slice(b * NB // 2, (b + 1) * NB // 2)
                return dve.scalar_tensor_tensor(out=y_out[:, k, rows, :], in0=post_d[:, rows, :], scalar=0.0,
                                                in1=xh[:, k, rows, :], op0=ALU.max, op1=ALU.add)

            def add_edge_rows(t):
                k = t.slot(TURN)
                dve.wait_ge(h_ready, t.at(TURN) + 1)
                dve.tensor_tensor(xh_dst[:, k, :, :], g_in[:, k, EB:2 * EB, 0:F], hg_row[:, k, EB:2 * EB, :], ALU.add
                                  ).then_inc(xh_dst_ready, 1)

            def combine(t, a):
                k = t.slot(POST)
                for c in range(EB):
                    last = dve.scalar_tensor_tensor(
                        out=comb[:, a, c, :], in0=post_e[:, c, a, :], scalar=gain[:, k, a, c:c + 1],
                        in1=comb[:, a - 1, c, :] if a else beta_b[:, :], op0=ALU.mult, op1=ALU.add)
                last.then_inc(comb_step, 1)

            def body(t):
                if t.has(NORM):
                    k = t.slot(NORM)
                    dve.wait_ge(x_loaded[k], 16 * (t.lap(NORM) + 1))
                    for j in range(NB):
                        dve.bn_stats(stats[:, k, j, :], x_in[:, k, j, :])
                    dve.wait_ge(g_loaded[k], 32 * EB * (t.lap(NORM) + 1))
                    for c in range(2 * EB):
                        last = dve.bn_stats(stats[:, k, NB + c, :], g_in[:, k, c, 0:F])
                    last.then_inc(mean_step, 1)
                if t.has(POST):
                    j = t.slot(POST)
                    dve.wait_ge(xh_ready, t.at(POST) + 1)
                    dve.wait_ge(xh_dst_ready, t.at(POST) + 1)
                    dve.wait_ge(gain_ready, t.at(POST) + 1)
                    if t.reused(POST):
                        dve.wait_ge(y_stored[j], 16 * t.lap(POST))
                        dve.wait_ge(y_scattered[j], 32 * t.lap(POST))
                if t.has(MSG):
                    dve.wait_ge(edge_loaded[t.slot(MSG)], 32 * (t.lap(MSG) + 1))
                if t.has(NORM):
                    dve.wait_ge(mean_step, 3 * t.at(NORM) + 1)
                    dve.tensor_tensor(mdiff[:, 0, :], stats[:, k, :, 1], stats[:, k, :, 4], ALU.subtract)
                    dve.tensor_tensor(mean2[:, k, :], stats[:, k, :, 1], stats[:, k, :, 4], ALU.add)
                    dve.tensor_tensor(mdiff[:, 1, :], stats[:, k, :, 2], stats[:, k, :, 5], ALU.add).then_inc(mean_step, 1)
                if t.has(TURN):
                    j, tiles = t.slot(TURN), bass.ds(t.at(TURN) * EB, EB)
                    dve.tensor_copy(gain[:, j, 0, :], g_in[:, j, EB:2 * EB, F])
                    dve.tensor_tensor(gain[:, j, 1, :], g_in[:, j, EB:2 * EB, F], amp_att[:, 0, tiles], ALU.mult)
                if t.has(NORM):
                    dve.wait_ge(mean_step, 3 * t.at(NORM) + 2)
                    dve.tensor_tensor(mdiff[:, 2, :], mdiff[:, 0, :], mdiff[:, 0, :], ALU.mult).then_inc(mean_step, 1)
                if t.has(TURN):
                    dve.tensor_tensor(gain[:, j, 2, :], g_in[:, j, EB:2 * EB, F], amp_att[:, 1, tiles], ALU.mult
                                      ).then_inc(gain_ready, 1)
                if t.has(NORM):
                    dve.wait_ge(mean_step, 3 * t.at(NORM) + 3)
                    dve.scalar_tensor_tensor(out=var[:, k, :], in0=mdiff[:, 2, :], scalar=F / 4.0, in1=mdiff[:, 1, :],
                                             op0=ALU.mult, op1=ALU.add).then_inc(var_ready, 1)
                    if not t.after(NORM):
                        scale_weights()
                    if not t.looped and t.c == NORM + 1:
                        split_bias()
                if t.has(TURN) and t.after(TURN):
                    add_edge_rows(t)
                if t.has(NORM):
                    dve.wait_ge(std_ready, t.at(NORM) + 1)
                    dve.reciprocal(rstd[:, k, :], std[:, k, :]).then_inc(rstd_ready, 1)
                if t.has(NORM):
                    dve.wait_ge(rstd_ready, t.at(NORM) + 1)
                    dve.scalar_tensor_tensor(out=nmean[:, k, :], in0=mean2[:, k, :], scalar=-0.5, in1=rstd[:, k, :],
                                             op0=ALU.mult, op1=ALU.mult).then_inc(norm_ready, 1)
                    if not t.after(NORM):
                        dve.wait_ge(set_pe, 4)
                        chain(dve.tensor_copy(amp_att[:, :, :], msg_ps[:, 0:2 * P].rearrange("p (b t) -> p b t", b=2)[:, :, 0:ET]))
                        mark(set_ready)
                    if not t.looped and t.c == TURN:
                        add_edge_rows(t)
                    if not t.looped and t.c == NORM + 2:
                        scale_rest()
                if t.has(POST):
                    dve.wait_ge(post_d_ready, t.at(POST) + 1)
                    finish_rows(t, 0)
                    finish_rows(t, 1).then_inc(y_out_ready, 1)
                if t.has(POST):
                    dve.wait_ge(post_e_ready, t.at(POST) + 1)
                    combine(t, 0)
                    dve.wait_ge(comb_step, 3 * t.at(POST) + 1)
                    combine(t, 1)
                if t.has(MSG):
                    k, before = t.slot(MSG), t.slot(MSG + 1)
                    end = slice(EW - 1, EW)
                    dve.wait_ge(msg_ready, t.at(MSG) + 1)
                    if t.after(MSG):
                        dve.wait_ge(agg_ready, t.at(MSG))
                    dve.tensor_tensor_scan(seg_sum[:, k, :], flags[:, k, 0, :], msg_ps[:, 0:EW],
                                           seg_sum[:, before, end], ALU.mult, ALU.add).then_inc(scanned, 1)
                if t.has(POST):
                    dve.wait_ge(comb_step, 3 * t.at(POST) + 2)
                    combine(t, 2)
                if t.has(MSG):
                    dve.tensor_tensor_scan(seg_agg[:, k, 1, :], flags[:, k, 1, :], msg_ps[:, 0:EW],
                                           seg_agg[:, before, 1, end], ALU.min, ALU.max)
                    dve.tensor_tensor_scan(seg_agg[:, k, 2, :], flags[:, k, 2, :], msg_ps[:, 0:EW],
                                           seg_agg[:, before, 2, end], ALU.max, ALU.min)
                    dve.wait_ge(scanned, t.at(MSG) + 1)
                    dve.tensor_tensor(seg_agg[:, k, 0, :], seg_sum[:, k, :], rdeg[:, k, :], ALU.mult).then_inc(agg_ready, 1)
                if t.has(POST):
                    j = t.slot(POST)
                    dve.wait_ge(comb_step, 3 * t.at(POST) + 3)
                    dve.scalar_tensor_tensor(out=y_edge[:, j, :, :], in0=comb[:, 2, :, :], scalar=0.0,
                                             in1=xh_dst[:, j, :, :], op0=ALU.max, op1=ALU.add).then_inc(y_edge_ready, 1)
                if not t.looped and t.c == NORM + 2:
                    list_scatters()

            run_steps(dve, NORM, POST, body)


def kernel(x, src, dst, edge_attr_16, node_vec1, L0_gnn_W_pre, L0_gnn_b_pre, L0_gnn_W_post, L0_gnn_b_post,
           L0_gnn_bn_gamma, L0_gnn_bn_beta):
    import numpy as np
    import concourse.bacc as bacc
    from concourse.bass_utils import run_bass_kernel_spmd

    x, src, dst, e, s = (np.ascontiguousarray(a) for a in (x, src, dst, edge_attr_16, node_vec1))
    dst_ext = np.full(EPAD + 2, PAD, dst.dtype)
    dst_ext[0] = dst_ext[-1] = -1
    dst_ext[1:E + 1] = dst
    src_pad = np.zeros(EPAD, src.dtype)
    src_pad[:E] = src
    e_t = np.zeros((ED, EPAD), e.dtype)
    e_t[:, :E] = e.T

    def by_slot(a):
        return np.ascontiguousarray(a.reshape(ET, P).T)

    arrays = {
        "x": x, "x_s": np.ascontiguousarray(np.concatenate([x, s], axis=1)), "snorm": s, "dst_ext": dst_ext,
        "dst_col": by_slot(dst_ext[1:EPAD + 1]), "next_col": by_slot(dst_ext[2:EPAD + 2]), "src_col": by_slot(src_pad),
        "e_t": e_t, "e_row": e, "w_pre": L0_gnn_W_pre, "b_pre": L0_gnn_b_pre, "w_post": L0_gnn_W_post, "b_post": L0_gnn_b_post,
        "gamma": L0_gnn_bn_gamma, "beta": L0_gnn_bn_beta,
    }
    arrays = {name: np.ascontiguousarray(a) for name, a in arrays.items()}
    nc = bacc.Bacc("TRN2", target_bir_lowering=False, num_devices=1)
    args = [nc.dram_tensor(name, a.shape, mybir.dt.from_np(a.dtype), kind="ExternalInput").ap()
            for name, a in arrays.items()]
    out = nc.dram_tensor("out", (N, F), F32, kind="ExternalOutput").ap()
    gnn_layer(nc, *args, out)
    return run_bass_kernel_spmd(nc, [arrays], core_ids=[0]).results[0]["out"]
```
